# Optimizing a Trainium2 kernel written in Bass

```python
import numpy as np
import jax
import jax.numpy as jnp

def _softmax(x, axis=-1):
    return jax.nn.softmax(x, axis=axis)

def _gelu(x):
    return jax.nn.gelu(x, approximate=True)

def _silu(x):
    return jax.nn.silu(x)

def _sigmoid(x):
    return jax.nn.sigmoid(x)

def _layernorm(x, axis=-1, eps=1e-05):
    m = jnp.mean(x, axis=axis, keepdims=True)
    v = jnp.var(x, axis=axis, keepdims=True)
    return (x - m) / jnp.sqrt(v + eps)

def _scatter_add(tgt, idx, src, axis=0):
    return tgt.at[idx].add(src)

def _segment_sum(src, seg, n):
    return jax.ops.segment_sum(src, seg, n)
kernel_name = 'mk_audio_tower_d1_tok_audfeat512_r4_78ec57'

def setup_inputs(seed: int=0):
    np.random.seed(seed)
    _w = jnp.asarray

    def _rec_inputs():
        import jax
        import jax.numpy as jnp
        _rk = jax.random.key(seed)
        x = -0.000612844 + 1.00049 * jax.random.normal(jax.random.fold_in(_rk, 1), (32, 100, 512), jnp.float32)
        return x
    x = _rec_inputs()

    def _L0_tok_setup():
        import jax, jax.numpy as jnp
        import numpy as np
        B, C_IN, T = (16, 100, 512)
        DIM, INTER, L = (128, 384, 8)
        EPS = 1e-06

        def layer_norm(x, w, b):
            mu = x.mean(-1, keepdims=True)
            var = ((x - mu) ** 2).mean(-1, keepdims=True)
            return (x - mu) * jax.lax.rsqrt(var + EPS) * w + b

        def conv1d(x, w, b, groups=1):
            y = jax.lax.conv_general_dilated(x, w, (1,), [(3, 3)], dimension_numbers=('NCH', 'OIH', 'NCH'), feature_group_count=groups)
            return y + b[None, :, None]
        key = jax.random.key(seed)
        ks = jax.random.split(key, 8)
        s = lambda k, shape, sc=0.02: jax.random.normal(k, shape, jnp.float32) * sc
        return {'x': jax.random.normal(ks[0], (B, C_IN, T), jnp.float32), 'embed_w': s(ks[1], (DIM, C_IN, 7)), 'embed_b': jnp.zeros((DIM,), jnp.float32), 'norm_w': jnp.ones((DIM,), jnp.float32), 'norm_b': jnp.zeros((DIM,), jnp.float32), 'dw_w': s(ks[2], (L, DIM, 1, 7)), 'dw_b': jnp.zeros((L, DIM), jnp.float32), 'ln_w': jnp.ones((L, DIM), jnp.float32), 'ln_b': jnp.zeros((L, DIM), jnp.float32), 'w1': s(ks[3], (L, INTER, DIM)), 'b1': jnp.zeros((L, INTER), jnp.float32), 'w2': s(ks[4], (L, DIM, INTER)), 'b2': jnp.zeros((L, DIM), jnp.float32), 'gamma': jnp.full((L, DIM), 1.0 / L, jnp.float32), 'final_ln_w': jnp.ones((DIM,), jnp.float32), 'final_ln_b': jnp.zeros((DIM,), jnp.float32)}
    _L0_tok_all = _L0_tok_setup()
    _L0_tok_in = {k: v for k, v in _L0_tok_all.items() if k in ('embed_w', 'embed_b', 'norm_w', 'norm_b', 'dw_w', 'dw_b', 'ln_w', 'ln_b', 'w1', 'b1', 'w2', 'b2', 'gamma', 'final_ln_w', 'final_ln_b')}
    del _L0_tok_all

    def _L0_attn_setup():
        import jax, jax.numpy as jnp
        import numpy as np
        DIM = 128
        HEADS = 8
        HEAD_DIM = DIM // HEADS
        key = jax.random.key(seed)
        ks = jax.random.split(key, 9)
        B, T, C = (8, 2048, DIM)
        s = 1.0 / np.sqrt(C)
        x = jax.random.normal(ks[0], (B, T, C), dtype=jnp.float32)
        Wq = jax.random.uniform(ks[1], (C, C), jnp.float32, -s, s)
        bq = jax.random.uniform(ks[2], (C,), jnp.float32, -s, s)
        Wk = jax.random.uniform(ks[3], (C, C), jnp.float32, -s, s)
        bk = jax.random.uniform(ks[4], (C,), jnp.float32, -s, s)
        Wv = jax.random.uniform(ks[5], (C, C), jnp.float32, -s, s)
        bv = jax.random.uniform(ks[6], (C,), jnp.float32, -s, s)
        Wo = jax.random.uniform(ks[7], (C, C), jnp.float32, -s, s)
        bo = jax.random.uniform(ks[8], (C,), jnp.float32, -s, s)
        return {'x': x, 'Wq': Wq, 'bq': bq, 'Wk': Wk, 'bk': bk, 'Wv': Wv, 'bv': bv, 'Wo': Wo, 'bo': bo}
    _L0_attn_all = _L0_attn_setup()
    _L0_attn_in = {k: v for k, v in _L0_attn_all.items() if k in ('Wq', 'bq', 'Wk', 'bk', 'Wv', 'bv', 'Wo', 'bo')}
    del _L0_attn_all

    def _L0_ffn_setup():
        import jax, jax.numpy as jnp
        import numpy as np
        import math
        D_MODEL = 128
        N_EXPERTS = 128
        TOP_K = 8
        N_HEADS = 8
        D_KEYS = 128
        HALF = D_KEYS // 2
        N_BATCH, T_SEQ = (2, 512)
        key = jax.random.key(seed)
        k1, k2, k3, k4, k5, k6 = jax.random.split(key, 6)
        queries = jax.random.normal(k1, (N_BATCH, T_SEQ, D_MODEL), dtype=jnp.float32)
        bound_q = 1.0 / math.sqrt(D_MODEL)
        Wq = jax.random.uniform(k2, (N_HEADS * D_KEYS, D_MODEL), minval=-bound_q, maxval=bound_q, dtype=jnp.float32)
        bq = jax.random.uniform(k3, (N_HEADS * D_KEYS,), minval=-bound_q, maxval=bound_q, dtype=jnp.float32)
        bound_k = 1.0 / math.sqrt(HALF)
        keys = jax.random.uniform(k4, (N_HEADS, 2, N_EXPERTS, HALF), minval=-bound_k, maxval=bound_k, dtype=jnp.float32)
        std = D_MODEL ** (-0.5)
        w_down_embed = std * jax.random.normal(k5, (N_EXPERTS * N_EXPERTS, D_MODEL), dtype=jnp.float32)
        w_up_embed = std * jax.random.normal(k6, (N_EXPERTS * N_EXPERTS, D_MODEL), dtype=jnp.float32)
        return {'queries': queries, 'Wq': Wq, 'bq': bq, 'keys': keys, 'w_down_embed': w_down_embed, 'w_up_embed': w_up_embed}
    _L0_ffn_all = _L0_ffn_setup()
    _L0_ffn_in = {k: v for k, v in _L0_ffn_all.items() if k in ('Wq', 'bq', 'keys', 'w_down_embed', 'w_up_embed')}
    del _L0_ffn_all
    return {'x': x, 'L0_tok_embed_w': _L0_tok_in['embed_w'], 'L0_tok_embed_b': _L0_tok_in['embed_b'], 'L0_tok_norm_w': _L0_tok_in['norm_w'], 'L0_tok_norm_b': _L0_tok_in['norm_b'], 'L0_tok_dw_w': _L0_tok_in['dw_w'], 'L0_tok_dw_b': _L0_tok_in['dw_b'], 'L0_tok_ln_w': _L0_tok_in['ln_w'], 'L0_tok_ln_b': _L0_tok_in['ln_b'], 'L0_tok_w1': _L0_tok_in['w1'], 'L0_tok_b1': _L0_tok_in['b1'], 'L0_tok_w2': _L0_tok_in['w2'], 'L0_tok_b2': _L0_tok_in['b2'], 'L0_tok_gamma': _L0_tok_in['gamma'], 'L0_tok_final_ln_w': _L0_tok_in['final_ln_w'], 'L0_tok_final_ln_b': _L0_tok_in['final_ln_b'], 'L0_attn_Wq': _L0_attn_in['Wq'], 'L0_attn_bq': _L0_attn_in['bq'], 'L0_attn_Wk': _L0_attn_in['Wk'], 'L0_attn_bk': _L0_attn_in['bk'], 'L0_attn_Wv': _L0_attn_in['Wv'], 'L0_attn_bv': _L0_attn_in['bv'], 'L0_attn_Wo': _L0_attn_in['Wo'], 'L0_attn_bo': _L0_attn_in['bo'], 'L0_ffn_Wq': _L0_ffn_in['Wq'], 'L0_ffn_bq': _L0_ffn_in['bq'], 'L0_ffn_keys': _L0_ffn_in['keys'], 'L0_ffn_w_down_embed': _L0_ffn_in['w_down_embed'], 'L0_ffn_w_up_embed': _L0_ffn_in['w_up_embed']}

def reference(x, L0_tok_embed_w, L0_tok_embed_b, L0_tok_norm_w, L0_tok_norm_b, L0_tok_dw_w, L0_tok_dw_b, L0_tok_ln_w, L0_tok_ln_b, L0_tok_w1, L0_tok_b1, L0_tok_w2, L0_tok_b2, L0_tok_gamma, L0_tok_final_ln_w, L0_tok_final_ln_b, L0_attn_Wq, L0_attn_bq, L0_attn_Wk, L0_attn_bk, L0_attn_Wv, L0_attn_bv, L0_attn_Wo, L0_attn_bo, L0_ffn_Wq, L0_ffn_bq, L0_ffn_keys, L0_ffn_w_down_embed, L0_ffn_w_up_embed):
    import jax
    import jax.numpy as jnp

    def _L0_tok_ref(x, embed_w, embed_b, norm_w, norm_b, dw_w, dw_b, ln_w, ln_b, w1, b1, w2, b2, gamma, final_ln_w, final_ln_b):
        import jax, jax.numpy as jnp
        import numpy as np
        B, C_IN, T = (16, 100, 512)
        DIM, INTER, L = (128, 384, 8)
        EPS = 1e-06

        def layer_norm(x, w, b):
            mu = x.mean(-1, keepdims=True)
            var = ((x - mu) ** 2).mean(-1, keepdims=True)
            return (x - mu) * jax.lax.rsqrt(var + EPS) * w + b

        def conv1d(x, w, b, groups=1):
            y = jax.lax.conv_general_dilated(x, w, (1,), [(3, 3)], dimension_numbers=('NCH', 'OIH', 'NCH'), feature_group_count=groups)
            return y + b[None, :, None]
        h = conv1d(x, embed_w, embed_b)
        h = layer_norm(h.transpose(0, 2, 1), norm_w, norm_b).transpose(0, 2, 1)

        def block(h, p):
            dw, db, lw, lb, W1, B1, W2, B2, g = p
            y = conv1d(h, dw, db, groups=DIM)
            y = y.transpose(0, 2, 1)
            y = layer_norm(y, lw, lb)
            y = jnp.einsum('btd,fd->btf', y, W1) + B1
            y = jax.nn.gelu(y, approximate=False)
            y = jnp.einsum('btf,df->btd', y, W2) + B2
            y = (g * y).transpose(0, 2, 1)
            return (h + y, None)
        h, _ = jax.lax.scan(block, h, (dw_w, dw_b, ln_w, ln_b, w1, b1, w2, b2, gamma))
        return layer_norm(h.transpose(0, 2, 1), final_ln_w, final_ln_b)

    def _L0_attn_ref(x, Wq, bq, Wk, bk, Wv, bv, Wo, bo):
        import jax, jax.numpy as jnp
        import numpy as np
        DIM = 128
        HEADS = 8
        HEAD_DIM = DIM // HEADS
        B, T, C = x.shape
        H, D = (HEADS, HEAD_DIM)

        def proj(W, b):
            return (x @ W.T + b).reshape(B, T, H, D).transpose(0, 2, 1, 3)
        Q = proj(Wq, bq)
        K = proj(Wk, bk)
        V = proj(Wv, bv)
        Q = jax.nn.elu(Q) + 1.0
        K = jax.nn.elu(K) + 1.0
        KV = jnp.einsum('bhnd,bhne->bhde', K, V)
        Q_KV = jnp.einsum('bhnd,bhde->bhne', Q, KV)
        K_sum = K.sum(axis=2)
        normalizer = jnp.einsum('bhnd,bhd->bhn', Q, K_sum)
        out = Q_KV / (normalizer[..., None] + 1e-06)
        out = out.transpose(0, 2, 1, 3).reshape(B, T, C)
        out = out @ Wo.T + bo
        return out

    def _L0_ffn_ref(queries, Wq, bq, keys, w_down_embed, w_up_embed):
        import jax, jax.numpy as jnp
        import numpy as np
        import math
        D_MODEL = 128
        N_EXPERTS = 128
        TOP_K = 8
        N_HEADS = 8
        D_KEYS = 128
        HALF = D_KEYS // 2
        N_BATCH, T_SEQ = (2, 512)
        N, T, D = queries.shape
        H, E, K = (N_HEADS, N_EXPERTS, TOP_K)
        q_tok = queries.reshape(-1, D)
        qh = q_tok @ Wq.T + bq
        qh = qh.reshape(-1, H, 2, HALF)
        sub_scores = jnp.einsum('nhcf,hcef->nhce', qh, keys)
        s, idx = jax.lax.top_k(sub_scores, K)
        all_scores = (s[:, :, 0, :, None] + s[:, :, 1, None, :]).reshape(-1, H, K * K)
        all_idx = (idx[:, :, 0, :, None] * E + idx[:, :, 1, None, :]).reshape(-1, H, K * K)
        best_s, best_pos = jax.lax.top_k(all_scores, K)
        indices = jnp.take_along_axis(all_idx, best_pos, axis=-1)
        w_down = w_down_embed[indices]
        w_up = w_up_embed[indices]
        x = jnp.einsum('nd,nhkd->nhk', q_tok, w_down)
        x = jax.nn.gelu(x)
        vals = x * jax.nn.softmax(best_s, axis=-1)
        out = jnp.einsum('nhk,nhkd->nd', vals, w_up)
        return out.reshape(N, T, D)
    h = _L0_tok_ref(x, L0_tok_embed_w, L0_tok_embed_b, L0_tok_norm_w, L0_tok_norm_b, L0_tok_dw_w, L0_tok_dw_b, L0_tok_ln_w, L0_tok_ln_b, L0_tok_w1, L0_tok_b1, L0_tok_w2, L0_tok_b2, L0_tok_gamma, L0_tok_final_ln_w, L0_tok_final_ln_b)
    h = h + _L0_attn_ref(_layernorm(h, axis=-1), L0_attn_Wq, L0_attn_bq, L0_attn_Wk, L0_attn_bk, L0_attn_Wv, L0_attn_bv, L0_attn_Wo, L0_attn_bo)
    h = h + _L0_ffn_ref(_layernorm(h, axis=-1), L0_ffn_Wq, L0_ffn_bq, L0_ffn_keys, L0_ffn_w_down_embed, L0_ffn_w_up_embed)
    return h

_drawn_inputs = setup_inputs


def setup_inputs(seed=0):
    import zlib

    import numpy as np

    out = dict(_drawn_inputs(seed))
    spreads = {'L0_tok_embed_b': (0.0, 0.1),
     'L0_tok_norm_w': (1.0, 0.2),
     'L0_tok_norm_b': (0.0, 0.1),
     'L0_tok_dw_b': (0.0, 0.404),
     'L0_tok_ln_w': (1.0, 0.6),
     'L0_tok_ln_b': (0.0, 0.8),
     'L0_tok_b1': (0.0, 0.706),
     'L0_tok_b2': (0.0, 0.1),
     'L0_tok_gamma': (0.125, 0.6),
     'L0_tok_final_ln_w': (1.0, 0.2),
     'L0_tok_final_ln_b': (0.0, 0.1)}
    factors = {'L0_tok_dw_w': 5.126,
     'L0_tok_w1': 3.209,
     'L0_attn_Wq': 31.261,
     'L0_attn_bq': 64.0,
     'L0_attn_Wk': 24.118,
     'L0_attn_bk': 64.0}
    for name, (base, spread) in spreads.items():
        noise = np.random.default_rng([zlib.crc32(name.encode()), seed]).standard_normal(out[name].shape)
        drawn = base * np.exp(spread * noise) if base else spread * noise
        out[name] = jnp.asarray(drawn.astype(out[name].dtype))
    for name, factor in factors.items():
        out[name] = (out[name] * factor).astype(out[name].dtype)
    return out
```

```python
from contextlib import ExitStack

import concourse.bass as bass
from concourse import mybir

ALU = mybir.AluOpType
ACT = mybir.ActivationFunctionType
AX = mybir.AxisListType
F32 = mybir.dt.float32
U32 = mybir.dt.uint32

P = 128
BATCH, CIN, SEQ = 32, 100, 512
TAPS, PAD = 7, 3
DIM, INTER, LAYERS = 128, 384, 8
FBLK = INTER // P
HEADS, HDIM = 8, 16
PH, HALF, TOPK = 8, 64, 8
NKEY = 128
TILES = SEQ // P
SLOTS = TILES * PH
RING = 4
CHUNK = 4 * NKEY
CHUNKS = PH // 2
TAIL = 7 + 1
CAND = 8 + 4 + 2 * 2 + 4
LNS = LAYERS + 4
LN_FINAL, LN_ATTN, LN_PEER = LAYERS + 1, LAYERS + 2, LAYERS + 3

FRONT = [[("ln", 0)]]
for _l in range(LAYERS):
    FRONT += [[("ln", _l + 1)], [("mlp", _l)]]
    if _l in (2, 5):
        FRONT += [[]]
FRONT += [[("ln", LN_FINAL)], [("ln", LN_ATTN)], [("qkv", 0), ("elu", 0)], [("kv", 0), ("mix", 0)],
          [("out", 0), ("ln", LN_PEER)]]
assert len(FRONT) == 3 * PH


def front_at(slot):
    return FRONT[slot] if slot < len(FRONT) else []


def build(nc, t, out):
    with ExitStack() as ctx:
        def sb(name, shape, dt=F32):
            return ctx.enter_context(nc.sbuf_tensor(name, shape, dt))

        def sem(name):
            return ctx.enter_context(nc.semaphore(name))

        def bank(name):
            return ctx.enter_context(nc.psum_tensor(name, [P, 512], F32))

        ident = sb("ident", [P, P])
        center = sb("center", [P, P])
        mean_w = sb("mean_w", [P, P])
        ones = sb("ones", [P, P])
        head_mask = sb("head_mask", [P, P])
        cand_iota = sb("cand_iota", [P, CAND])
        eps = sb("eps", [P, 3])
        emb_w = sb("emb_w", [CIN, TAPS, DIM])
        dw = sb("dw", [P, LAYERS * TAPS, DIM])
        w1 = sb("w1", [P, LAYERS, INTER])
        w2 = sb("w2", [P, LAYERS * FBLK, DIM])
        wq = sb("wq", [P, DIM])
        wkv = sb("wkv", [P, 2 * DIM])
        wo = sb("wo", [P, DIM])
        score_w = sb("score_w", [P, 2 * PH * NKEY])
        score_b = sb("score_b", [1, 2 * PH * NKEY])
        kv_b = sb("kv_b", [P, 2 * DIM])
        conv_b = sb("conv_b", [P, LNS])
        ln_b1 = sb("ln_b1", [P, LAYERS * FBLK])
        gamma_b2 = sb("gamma_b2", [P, LAYERS])
        vecs = sb("vecs", [P, 6])
        gamma = sb("gamma", [P, LAYERS])
        row_b = sb("row_b", [1, 2 * DIM])

        xin = sb("xin", [CIN, SEQ + 2 * PAD])
        h = sb("h", [P, SEQ + 2 * PAD])
        hin = h[:, PAD:PAD + SEQ]
        square = sb("square", [P, SEQ])
        std = sb("std", [P, SEQ])
        rstd = sb("rstd", [P, SEQ])
        xhat = sb("xhat", [P, SEQ])
        hb = sb("hb", [P, SEQ])
        act = sb("act", [P, FBLK, SEQ])
        hf = sb("hf", [P, SEQ])
        h2 = sb("h2", [P, SEQ])
        qc = sb("qc", [P, SEQ])
        q_exp = sb("q_exp", [P, SEQ])
        q_pos = sb("q_pos", [P, SEQ])
        q_elu = sb("q_elu", [P, SEQ])
        kvt = sb("kvt", [P, TILES, 2 * DIM + 1])
        k_exp = sb("k_exp", [P, TILES, DIM])
        k_pos = sb("k_pos", [P, TILES, DIM])
        k_elu = sb("k_elu", [P, TILES, DIM])
        kv_sum = sb("kv_sum", [P, 1])
        kv_m = sb("kv_m", [P, P])
        ks_m = sb("ks_m", [P, P])
        mixed = sb("mixed", [P, SEQ])

        ring = sb("ring", [P, RING, TOPK, 2 * DIM])
        tok = sb("tok", [P, 2, 2 * DIM])
        expert = sb("expert", [P, 2, PH * TOPK], U32)
        weight = sb("weight", [P, 2, PH * TOPK])
        half = sb("half", [P, 2, 2, 2, TOPK])
        half_u = sb("half_u", [P, 2, 2, TOPK], U32)
        cand = sb("cand", [P, 2, 2, CAND])
        best = sb("best", [P, PH, TOPK])
        pos = sb("pos", [P, 2, TOPK], U32)
        hit = sb("hit", [P, 2 * TOPK, CAND])
        picked = sb("picked", [P, 2 * TOPK, CAND])
        shifted = sb("shifted", [P, PH, TOPK])
        expd = sb("expd", [P, PH, TOPK])
        total = sb("total", [P, PH])
        inv_total = sb("inv_total", [P, PH])
        dot = sb("dot", [P, 2, TOPK])
        dot2 = sb("dot2", [P, TOPK])
        cubic = sb("cubic", [P, TOPK])
        tanh_in = sb("tanh_in", [P, 2, TOPK])
        tanh = sb("tanh", [P, 2, TOPK])
        gated = sb("gated", [P, TOPK])
        val = sb("val", [P, TOPK])
        acc = sb("acc", [P, TOPK, DIM])
        summed = sb("summed", [P, DIM])
        outt = sb("outt", [P, 2, DIM])

        stage = ring[:, :, :, :].rearrange("p r k d -> p (r k d)")
        keys_s = stage[0:HALF, 0:2048].rearrange("p (c e) -> p c e", c=2 * PH)
        fwq_s = stage[0:HALF, 2048:4096].rearrange("p (c e) -> p c e", c=2 * PH)
        emb_s = stage[:, 4096:4096 + CIN * TAPS].rearrange("p (c k) -> p c k", k=TAPS)
        dw_s = stage[:, 4800:4800 + LAYERS * TAPS]
        cb_s = stage[:, 4864:4864 + LNS]
        lnw_s = stage[:, 4880:4880 + LAYERS]
        lnb_s = stage[:, 4888:4888 + LAYERS]
        b1_s = stage[:, 4896:4896 + LAYERS * FBLK]
        b2_s = stage[:, 4920:4920 + LAYERS]
        fbq_s = stage[0:HALF, 4928:4928 + 2 * PH]

        bank_a, bank_b = bank("bank_a"), bank("bank_b")
        bank_c = [bank(f"bank_c{i}") for i in range(3)]
        bank_s = [bank(f"bank_s{i}") for i in range(2)]
        bank_t = bank("bank_t")

        (loaded, masks, consts, prep_pe, prep_cp, prep_dve, ready) = map(sem, (
            "loaded", "masks", "consts", "prep_pe", "prep_cp", "prep_dve", "ready"))
        x_loaded = sem("x_loaded")
        centred, squared, varied, rooted, normed = map(sem, ("centred", "squared", "varied", "rooted", "normed"))
        affine, hidden, gelued, biased, projected, added = map(sem, (
            "affine", "hidden", "gelued", "biased", "projected", "added"))
        qkv_made, clamped, exped, elued, kv_summed, kv_masked, mix_made, mix_done, out_made, h2_done = map(sem, (
            "qkv_made", "clamped", "exped", "elued", "kv_summed", "kv_masked", "mix_made", "mix_done",
            "out_made", "h2_done"))
        scored, listed, turned, tok_ready, tok_free = map(sem, (
            "scored", "listed", "turned", "tok_ready", "tok_free"))
        chosen, shift_done, exp_done = map(sem, ("chosen", "shift_done", "exp_done"))
        landed = [sem(f"landed{i}") for i in range(RING)]
        rows_free, tanh_ready, tanh_done = map(sem, ("rows_free", "tanh_ready", "tanh_done"))
        out_ready, out_free = sem("out_ready"), [sem("out_free0"), sem("out_free1")]
        dve_done = sem("dve_done")
        passed = sem("passed")

        block = ctx.enter_context(nc.Block())

        LOADS = [
            (emb_s, t["embed_w"]), (dw_s, t["dw_w"]), (cb_s, t["conv_b"]), (lnw_s, t["ln_w"]),
            (lnb_s, t["ln_b"]), (b1_s, t["b1"]), (b2_s, t["b2"]), (fbq_s, t["ffn_bq"]),
            (keys_s, t["keys"]), (fwq_s, t["ffn_wq"]), (w1[:, :, :], t["w1"]), (w2[:, :, :], t["w2"]),
            (wq[:, :], t["wq"]), (wkv[:, :], t["wkv"]), (wo[:, :], t["wo"]), (vecs[:, :], t["vecs"]),
            (gamma[:, :], t["gamma"]), (row_b[:, :], t["bkv"]),
        ]
        N_LOADS = len(LOADS)

        @block.sync
        def _(sp):
            for dst, src in LOADS:
                sp.dma_start(dst, src).then_inc(loaded, 16)
            sp.wait_ge(masks, 1)
            sp.dma_start(xin[:, PAD:PAD + SEQ], t["x"][0]).then_inc(x_loaded, 16)

            def store(n, tile):
                sp.wait_ge(out_ready, n * TILES + (tile + 1))
                sp.dma_start(out[n, tile * P:(tile + 1) * P, :], outt[:, tile % 2, :])\
                  .then_inc(out_free[tile % 2], 16)

            with sp.Fori(0, BATCH - 1) as n:
                sp.wait_ge(centred, n * LNS + 1)
                sp.dma_start(xin[:, PAD:PAD + SEQ], t["x"][n + 1]).then_inc(x_loaded, 16)
                for tile in range(TILES):
                    store(n, tile)
            for tile in range(TILES):
                store(BATCH - 1, tile)
            for s in out_free:
                sp.wait_ge(s, 16 * BATCH * TILES // 2)

        @block.gpsimd
        def _(pool):
            pool.memset(xin[:, :], 0.0)
            pool.memset(h[:, :], 0.0).then_inc(masks, 1)
            pool.memset(ident[:, :], 0.0)
            pool.memset(mean_w[:, :], 1.0 / DIM)
            pool.memset(eps[:, 0:1], 1e-6)
            pool.memset(eps[:, 1:2], 1e-5)
            pool.memset(eps[:, 2:3], 0.0)
            pool.memset(kvt[:, :, 2 * DIM:2 * DIM + 1], 1.0)
            pool.iota(cand_iota[:, :], pattern=[[1, CAND]], base=0, channel_multiplier=0,
                      allow_small_or_imprecise_dtypes=True)
            pool.memset(head_mask[:, :], 1.0)
            pool.memset(ones[:, :], 1.0).then_inc(masks, 1)
            pool.wait_ge(masks, 2)
            pool.affine_select(out=ident[:, :], in_=ident[:, :], compare_op=ALU.not_equal, fill=1.0,
                               base=0, pattern=[[-1, P]], channel_multiplier=1).then_inc(masks, 1)
            by_head = head_mask[:, :].rearrange("p (g d) -> p g d", d=HDIM)
            pool.affine_select(out=by_head, in_=by_head, compare_op=ALU.is_ge, fill=0.0, base=0,
                               pattern=[[-HDIM, HEADS], [0, HDIM]], channel_multiplier=1).then_inc(masks, 1)
            pool.wait_ge(masks, 4)
            pool.affine_select(out=by_head, in_=by_head, compare_op=ALU.is_ge, fill=0.0, base=HDIM - 1,
                               pattern=[[HDIM, HEADS], [0, HDIM]], channel_multiplier=-1).then_inc(masks, 1)

            def gather(n, slot):
                tile, head = slot // PH, slot % PH
                pool.wait_ge(rows_free, n * SLOTS + (slot + 1))
                pool.wait_ge(chosen, n * (TILES * CHUNKS) + (tile * CHUNKS + head // 2 + 1))
                pool.sem_inc(passed, 1)
                for k in range(TOPK):
                    col = head * TOPK + k
                    pool.indirect_dma_start(
                        ring[:, slot % RING, k, :], None, t["experts"],
                        bass.IndirectOffsetOnAxis(ap=expert[:, tile % 2, col:col + 1], axis=0),
                    ).then_inc(landed[slot % RING], 16)

            pool.wait_ge(ready, 1)
            pool.sem_inc(passed, 1)
            with pool.Fori(0, BATCH) as n:
                for slot in range(SLOTS):
                    gather(n, slot)

        @block.tensor
        def _(pe):
            mm = nc.tensor.matmul
            pe.wait_ge(loaded, 16 * N_LOADS)
            pe.wait_ge(masks, 5)
            pe.wait_ge(consts, 1)
            for k in range(TAPS):
                dst = (bank_a if k < 4 else bank_b)[0:CIN, (k % 4) * DIM:(k % 4 + 1) * DIM]
                last = mm(dst, emb_s[:, :, k], center[:, :], start=True, stop=True)
            last.then_inc(prep_pe, 1)
            for l in range(LAYERS):
                for j in range(FBLK):
                    mm(bank_t[:, l * FBLK + j:l * FBLK + j + 1], w1[:, l, j * P:(j + 1) * P],
                       lnb_s[:, l:l + 1], start=True, stop=True)
            mm(bank_t[:, 32:32 + LNS], center[:, :], cb_s, start=True, stop=True)
            last = mm(bank_t[:, 128:128 + 2 * DIM], ones[0:1, :], row_b[:, :], start=True, stop=True)
            last.then_inc(prep_pe, 1)
            for c in range(CHUNKS):
                if c >= 2:
                    pe.wait_ge(prep_cp, c - 1)
                for i in range(4):
                    hc = 4 * c + i
                    mm(bank_s[c % 2][:, i * NKEY:(i + 1) * NKEY], fwq_s[:, hc, :], keys_s[:, hc, :],
                       start=True, stop=True)
                    last = mm(bank_c[c % 2][0:1, i * NKEY:(i + 1) * NKEY], fbq_s[:, hc:hc + 1],
                              keys_s[:, hc, :], start=True, stop=True)
                last.then_inc(prep_pe, 1)
            pe.wait_ge(ready, 1)

            def front(m, kind, k):
                if kind == "ln":
                    conv = k <= LAYERS
                    if k == 0:
                        pe.wait_ge(x_loaded, (m + 1) * 16)
                    elif k == 1 or k == LN_ATTN:
                        pe.wait_ge(affine, m * 2 + (1 if k == 1 else 2))
                    elif k == LN_PEER:
                        pe.wait_ge(h2_done, m + 1)
                    else:
                        pe.wait_ge(added, m * LAYERS + (k - 1))
                    if conv:
                        src = xin if k == 0 else h
                        for tap in range(TAPS):
                            w = emb_w[:, tap, :] if k == 0 else dw[:, (k - 1) * TAPS + tap, :]
                            last = mm(bank_a[:, :], w, src[:, tap:tap + SEQ], start=(tap == 0),
                                      stop=(tap == TAPS - 1))
                    else:
                        src = {LN_FINAL: hin, LN_ATTN: hf[:, :], LN_PEER: h2[:, :]}[k]
                        last = mm(bank_a[:, :], center[:, :], src, start=True, stop=True)
                    last.then_inc(centred, 1)
                    pe.wait_ge(squared, m * LNS + (k + 1))
                    mm(bank_b[:, :], mean_w[:, :], square[:, :], start=True, stop=True).then_inc(varied, 1)
                elif kind == "mlp":
                    pe.wait_ge(normed, m * LNS + (k + 2))
                    for j in range(FBLK):
                        mm(bank_c[j][:, :], w1[:, k, j * P:(j + 1) * P], xhat[:, :], start=True, stop=True)\
                            .then_inc(hidden, 1)
                    for j in range(FBLK):
                        pe.wait_ge(gelued, m * (LAYERS * FBLK) + (k * FBLK + j + 1))
                        last = mm(bank_b[:, :], w2[:, k * FBLK + j, :], act[:, j, :], start=(j == 0),
                                  stop=(j == FBLK - 1))
                    last.then_inc(projected, 1)
                elif kind == "qkv":
                    pe.wait_ge(normed, m * LNS + (LN_ATTN + 1))
                    mm(bank_c[0][:, :], wq[:, :], xhat[:, :], start=True, stop=True).then_inc(qkv_made, 1)
                    for i in range(TILES):
                        last = mm(bank_c[1 + i // 2][:, (i % 2) * 2 * DIM:(i % 2 + 1) * 2 * DIM],
                                  xhat[:, i * P:(i + 1) * P], wkv[:, :], start=True, stop=True)
                    last.then_inc(qkv_made, 1)
                elif kind == "kv":
                    pe.wait_ge(elued, m + 1)
                    for i in range(TILES):
                        last = mm(bank_b[:, 0:DIM + 1], k_elu[:, i, :], kvt[:, i, DIM:2 * DIM + 1],
                                  start=(i == 0), stop=(i == TILES - 1))
                    last.then_inc(kv_summed, 1)
                elif kind == "mix":
                    pe.wait_ge(kv_masked, m + 1)
                    mm(bank_c[2][:, :], ks_m[:, :], q_elu[:, :], start=True, stop=True)
                    mm(bank_c[1][:, :], kv_m[:, :], q_elu[:, :], start=True, stop=True).then_inc(mix_made, 1)
                elif kind == "out":
                    pe.wait_ge(mix_done, m + 1)
                    mm(bank_c[0][:, :], wo[:, :], mixed[:, :], start=True, stop=True).then_inc(out_made, 1)

            def scores(m, tile, c):
                if c == 0 and tile == 0:
                    pe.wait_ge(normed, m * LNS + LNS)
                pe.wait_ge(listed, m * (TILES * CHUNKS) + (tile * CHUNKS + c + 1))
                mm(bank_s[c % 2][:, :], qc[:, tile * P:(tile + 1) * P], score_w[:, c * CHUNK:(c + 1) * CHUNK],
                   start=True, stop=False)
                mm(bank_s[c % 2][:, :], ones[0:1, :], score_b[:, c * CHUNK:(c + 1) * CHUNK],
                   start=False, stop=True).then_inc(scored, 1)

            def turn(m, tile):
                pe.wait_ge(tok_ready, m * TILES + (tile + 1))
                for i, src in enumerate((qc, h2)):
                    last = nc.tensor.transpose(bank_t[:, i * DIM:(i + 1) * DIM],
                                               src[:, tile * P:(tile + 1) * P], ident[:, :])
                last.then_inc(turned, 1)

            def topk_slot(m, tile, part):
                if part % 2 == 0:
                    scores(m, tile, part // 2)
                if part == 5:
                    turn(m, tile)

            def slots(n, more):
                for slot in range(SLOTS):
                    tile, part = slot // PH, slot % PH
                    if tile + 1 < TILES:
                        topk_slot(n, tile + 1, part)
                    elif more:
                        topk_slot(n + 1, 0, part)
                    if more:
                        for kind, k in front_at(slot):
                            front(n + 1, kind, k)

            for stages in FRONT:
                for kind, k in stages:
                    front(0, kind, k)
            for part in range(PH):
                topk_slot(0, 0, part)
            with pe.Fori(0, BATCH - 1) as n:
                slots(n, True)
            slots(BATCH - 1, False)

        @block.scalar
        def _(act_e):
            activate = nc.scalar.activation
            act_e.wait_ge(prep_pe, 1)
            activate(emb_w[:, 0:4, :], bank_a[0:CIN, :].rearrange("p (k d) -> p k d", k=4), ACT.Copy)
            activate(emb_w[:, 4:7, :], bank_b[0:CIN, 0:3 * DIM].rearrange("p (k d) -> p k d", k=3), ACT.Copy)
            act_e.wait_ge(prep_dve, 1)
            activate(conv_b[:, :], bank_t[:, 32:32 + LNS], ACT.Copy)
            activate(kv_b[:, :], bank_t[:, 128:128 + 2 * DIM], ACT.Copy)
            for c in range(CHUNKS):
                act_e.wait_ge(prep_pe, 3 + c)
                activate(score_w[:, c * CHUNK:(c + 1) * CHUNK], bank_s[c % 2][:, :], ACT.Copy)
                activate(score_b[:, c * CHUNK:(c + 1) * CHUNK], bank_c[c % 2][0:1, :], ACT.Copy)\
                    .then_inc(prep_cp, 1)
            act_e.wait_ge(ready, 1)

            def front(m, kind, k):
                if kind == "ln":
                    act_e.wait_ge(centred, m * LNS + (k + 1))
                    activate(square[:, :], bank_a[:, :], ACT.Square, bias=conv_b[:, k:k + 1]).then_inc(squared, 1)
                    act_e.wait_ge(varied, m * LNS + (k + 1))
                    e = 0 if k <= LN_FINAL else 1
                    activate(std[:, :], bank_b[:, :], ACT.Sqrt, bias=eps[:, e:e + 1]).then_inc(rooted, 1)
                    if k in (0, LN_FINAL):
                        act_e.wait_ge(normed, m * LNS + (k + 1))
                        dst, v = (hin, 0) if k == 0 else (hf[:, :], 2)
                        activate(dst, xhat[:, :], ACT.Identity, bias=vecs[:, v + 1:v + 2],
                                 scale=vecs[:, v:v + 1]).then_inc(affine, 1)
                elif kind == "mlp":
                    if k == 0:
                        act_e.wait_ge(affine, m * 2 + 1)
                    else:
                        act_e.wait_ge(added, m * LAYERS + k)
                    activate(hb[:, :], hin, ACT.Identity, bias=gamma_b2[:, k:k + 1]).then_inc(biased, 1)
                    for j in range(FBLK):
                        act_e.wait_ge(hidden, m * (LAYERS * FBLK) + (k * FBLK + j + 1))
                        activate(act[:, j, :], bank_c[j][:, :], ACT.Gelu,
                                 bias=ln_b1[:, k * FBLK + j:k * FBLK + j + 1]).then_inc(gelued, 1)
                elif kind == "qkv":
                    act_e.wait_ge(clamped, m * 2 + 1)
                    activate(q_exp[:, :], q_exp[:, :], ACT.Exp).then_inc(exped, 1)
                    act_e.wait_ge(clamped, m * 2 + 2)
                    activate(k_exp[:, :, :], k_exp[:, :, :], ACT.Exp).then_inc(exped, 1)

            def tanh_slot(n, slot):
                act_e.wait_ge(tanh_ready, n * SLOTS + (slot + 1))
                activate(tanh[:, slot % 2, :], tanh_in[:, slot % 2, :], ACT.Tanh,
                         scale=0.7978845608028654).then_inc(tanh_done, 1)

            def topk_slot(m, tile, part):
                if part == 5:
                    act_e.wait_ge(turned, m * TILES + (tile + 1))
                    act_e.wait_ge(tok_free, m * TILES + (tile + 1))
                    activate(tok[:, tile % 2, :], bank_t[:, 0:2 * DIM], ACT.Copy).then_inc(tok_ready, 1)
                if part == PH - 1:
                    act_e.wait_ge(shift_done, m * TILES + (tile + 1))
                    activate(expd[:, :, :], shifted[:, :, :], ACT.Exp).then_inc(exp_done, 1)

            def slots(n, more):
                for slot in range(SLOTS):
                    tile, part = slot // PH, slot % PH
                    tanh_slot(n, slot)
                    if tile + 1 < TILES:
                        topk_slot(n, tile + 1, part)
                    elif more:
                        topk_slot(n + 1, 0, part)
                    if more:
                        for kind, k in front_at(slot):
                            front(n + 1, kind, k)

            for stages in FRONT:
                for kind, k in stages:
                    front(0, kind, k)
            for part in range(PH):
                topk_slot(0, 0, part)
            with act_e.Fori(0, BATCH - 1) as n:
                slots(n, True)
            slots(BATCH - 1, False)

        @block.vector
        def _(dve):
            v = nc.vector
            steps = [0]

            def step(ins):
                steps[0] += 1
                ins.then_inc(dve_done, 1)
                return steps[0]

            def after(n):
                dve.wait_ge(dve_done, n)

            def restart():
                dve.wait_ge(dve_done, steps[0])
                dve.sem_clear(dve_done)
                steps[0] = 0

            dve.wait_ge(masks, 5)
            v.tensor_tensor(center[:, :], ident[:, :], mean_w[:, :], ALU.subtract).then_inc(consts, 1)
            dve.wait_ge(loaded, 16 * N_LOADS)
            dve.wait_ge(consts, 1)
            for i in range(LAYERS * TAPS):
                v.tensor_scalar(dw[:, i, :], center[:, :], dw_s[:, i:i + 1], None, ALU.mult)
            v.tensor_tensor(gamma_b2[:, :], gamma[:, :], b2_s, ALU.mult)
            dve.wait_ge(prep_pe, 2)
            v.tensor_tensor(ln_b1[:, :], bank_t[:, 0:LAYERS * FBLK], b1_s, ALU.add).then_inc(prep_dve, 1)
            for l in range(LAYERS):
                last = v.tensor_scalar(w1[:, l, :], w1[:, l, :], lnw_s[:, l:l + 1], None, ALU.mult)
            last.then_inc(prep_dve, 1)
            dve.wait_ge(prep_dve, 2)
            dve.wait_ge(prep_cp, CHUNKS)
            dve.sem_inc(rows_free, RING)
            dve.sem_inc(listed, 2)
            dve.sem_inc(tok_free, 2)
            dve.sem_inc(tok_ready, 1)
            dve.sem_inc(ready, 1)

            def front(m, kind, k):
                if kind == "ln":
                    dve.wait_ge(rooted, m * LNS + (k + 1))
                    s = step(v.reciprocal(rstd[:, :], std[:, :]))
                    dst = qc if k == LN_PEER else xhat
                    after(s)
                    v.scalar_tensor_tensor(out=dst[:, :], in0=bank_a[:, :], scalar=conv_b[:, k:k + 1],
                                           in1=rstd[:, :], op0=ALU.add, op1=ALU.mult).then_inc(normed, 1)
                elif kind == "mlp":
                    dve.wait_ge(biased, m * LAYERS + (k + 1))
                    dve.wait_ge(projected, m * LAYERS + (k + 1))
                    v.scalar_tensor_tensor(out=hin, in0=bank_b[:, :], scalar=gamma[:, k:k + 1], in1=hb[:, :],
                                           op0=ALU.mult, op1=ALU.add).then_inc(added, 1)
                elif kind == "qkv":
                    dve.wait_ge(qkv_made, m * 2 + 2)
                    for j in range(2):
                        last = v.tensor_tensor(
                            kvt[:, 2 * j:2 * j + 2, 0:2 * DIM],
                            bank_c[1 + j][:, :].rearrange("p (i d) -> p i d", i=2),
                            kv_b[:, :].unsqueeze(1).broadcast_to([P, 2, 2 * DIM]), ALU.add)
                    biased_at = step(last)
                    q_in = bank_c[0][:, :]
                    v.tensor_scalar(q_exp[:, :], q_in, vecs[:, 4:5], 0.0, ALU.add, ALU.min).then_inc(clamped, 1)
                    after(biased_at)
                    v.tensor_scalar(k_exp[:, :, :], kvt[:, :, 0:DIM], 0.0, None, ALU.min).then_inc(clamped, 1)
                    step(v.tensor_scalar(q_pos[:, :], q_in, vecs[:, 4:5], 0.0, ALU.add, ALU.max))
                    step(v.tensor_scalar(k_pos[:, :, :], kvt[:, :, 0:DIM], 0.0, None, ALU.max))
                elif kind == "elu":
                    dve.wait_ge(exped, m * 2 + 2)
                    after(steps[0])
                    v.tensor_tensor(q_elu[:, :], q_exp[:, :], q_pos[:, :], ALU.add)
                    v.tensor_tensor(k_elu[:, :, :], k_exp[:, :, :], k_pos[:, :, :], ALU.add).then_inc(elued, 1)
                elif kind == "kv":
                    dve.wait_ge(kv_summed, m + 1)
                    s = step(v.tensor_copy(kv_sum[:, :], bank_b[:, DIM:DIM + 1]))
                    v.tensor_tensor(kv_m[:, :], head_mask[:, :], bank_b[:, 0:DIM], ALU.mult)
                    after(s)
                    v.tensor_scalar(ks_m[:, :], head_mask[:, :], kv_sum[:, :], None, ALU.mult)\
                        .then_inc(kv_masked, 1)
                elif kind == "mix":
                    dve.wait_ge(mix_made, m + 1)
                    s = step(v.tensor_scalar(q_pos[:, :], bank_c[2][:, :], 1e-6, None, ALU.add))
                    after(s)
                    s = step(v.reciprocal(q_exp[:, :], q_pos[:, :]))
                    after(s)
                    v.tensor_tensor(mixed[:, :], bank_c[1][:, :], q_exp[:, :], ALU.mult).then_inc(mix_done, 1)
                elif kind == "out":
                    dve.wait_ge(out_made, m + 1)
                    v.scalar_tensor_tensor(out=h2[:, :], in0=bank_c[0][:, :], scalar=vecs[:, 5:6], in1=hf[:, :],
                                           op0=ALU.add, op1=ALU.add).then_inc(h2_done, 1)

            def lists(m, tile, c):
                dve.wait_ge(scored, m * (TILES * CHUNKS) + (tile * CHUNKS + c + 1))
                dve.sem_inc(passed, 1)
                after(steps[0])
                for hd in range(2):
                    for cc in range(2):
                        cols = bank_s[c % 2][:, (2 * hd + cc) * NKEY:(2 * hd + cc + 1) * NKEY]
                        s = step(v.max(half[:, cc, hd, 0, :], cols))
                for hd in range(2):
                    for cc in range(2):
                        cols = bank_s[c % 2][:, (2 * hd + cc) * NKEY:(2 * hd + cc + 1) * NKEY]
                        after(s - 3 + 2 * hd + cc)
                        last = v.max_index(half_u[:, hd, cc, :], half[:, cc, hd, 0, :], cols)
                        if hd == 1 and cc == 1:
                            last.then_inc(listed, 1)

            def pairs(m, tile, c):
                dve.wait_ge(listed, m * (TILES * CHUNKS) + (tile * CHUNKS + c + 3))
                step(v.tensor_scalar(half[:, 0, :, 1, :], half_u[:, :, 0, :], float(NKEY), None, ALU.mult))
                s = step(v.tensor_scalar(half[:, 1, :, 1, :], half_u[:, :, 1, :], 1.0, None, ALU.mult))
                after(s)
                a = half[:, 0, :, :, :].rearrange("p h w k -> p (h w) k")
                b = half[:, 1, :, :, :].rearrange("p h w k -> p (h w) k")
                cd = cand[:, :, :, :].rearrange("p h w k -> p (h w) k")
                step(v.tensor_tensor(cd[:, :, 0:8], a[:, :, 0:1].broadcast_to([P, 4, 8]), b[:, :, 0:8], ALU.add))
                step(v.tensor_tensor(cd[:, :, 8:12], a[:, :, 1:2].broadcast_to([P, 4, 4]), b[:, :, 0:4], ALU.add))
                step(v.tensor_tensor(cd[:, :, 12:16].rearrange("p w (a b) -> p w a b", a=2),
                                     a[:, :, 2:4].unsqueeze(3).broadcast_to([P, 4, 2, 2]),
                                     b[:, :, 0:2].unsqueeze(2).broadcast_to([P, 4, 2, 2]), ALU.add))
                s = step(v.tensor_tensor(cd[:, :, 16:20], a[:, :, 4:8], b[:, :, 0:1].broadcast_to([P, 4, 4]),
                                         ALU.add))
                after(s)
                for hd in range(2):
                    s = step(v.max(best[:, 2 * c + hd, :], cand[:, hd, 0, :]))
                for hd in range(2):
                    after(s - 1 + hd)
                    last = step(v.max_index(pos[:, hd, :], best[:, 2 * c + hd, :], cand[:, hd, 0, :]))
                after(last)
                s = step(v.tensor_tensor(
                    hit[:, :, :], pos[:, :, :].rearrange("p h k -> p (h k)").unsqueeze(2).broadcast_to([P, 16, CAND]),
                    cand_iota[:, :].unsqueeze(1).broadcast_to([P, 16, CAND]), ALU.is_equal))
                after(s)
                s = step(v.tensor_tensor(
                    picked[:, :, :].rearrange("p (h k) c -> p h k c", h=2),
                    hit[:, :, :].rearrange("p (h k) c -> p h k c", h=2),
                    cand[:, :, 1, :].unsqueeze(2).broadcast_to([P, 2, TOPK, CAND]), ALU.mult))
                after(s)
                with nc.allow_low_precision(reason="one whole number under 2^14 and zeros"):
                    v.tensor_reduce(expert[:, tile % 2, 16 * c:16 * c + 16], picked[:, :, :], AX.X, ALU.add)\
                        .then_inc(chosen, 1)

            def soften(m, tile):
                after(steps[0])
                v.tensor_tensor(shifted[:, :, :], best[:, :, :], best[:, :, 0:1].broadcast_to([P, PH, TOPK]),
                                ALU.subtract).then_inc(shift_done, 1)
                dve.wait_ge(exp_done, m * TILES + (tile + 1))
                s = step(v.tensor_reduce(total[:, :], expd[:, :, :], AX.X, ALU.add))
                after(s)
                s = step(v.reciprocal(inv_total[:, :], total[:, :]))
                after(s)
                w = weight[:, tile % 2, :].rearrange("p (h k) -> p h k", h=PH)
                s = step(v.tensor_tensor(w, expd[:, :, :], inv_total[:, :].unsqueeze(2).broadcast_to([P, PH, TOPK]),
                                         ALU.mult))
                after(s)
                step(v.tensor_scalar(weight[:, tile % 2, :], weight[:, tile % 2, :], 0.5, None, ALU.mult))

            def topk_slot(m, tile, part):
                if part % 2 == 0:
                    lists(m, tile, part // 2)
                else:
                    pairs(m, tile, part // 2)
                if part == PH - 1:
                    soften(m, tile)

            def dots(n, slot):
                tile, r = slot // PH, slot % RING
                dve.wait_ge(landed[r], n * (SLOTS // RING * 16 * TOPK) + (slot // RING + 1) * 16 * TOPK)
                if slot % PH == 0:
                    dve.wait_ge(tok_ready, n * TILES + (tile + 2))
                d = dot[:, slot % 2, :]
                for k in range(TOPK):
                    s = step(v.tensor_tensor_reduce(ring[:, r, k, 0:DIM], ring[:, r, k, 0:DIM], tok[:, tile % 2, 0:DIM],
                                                    1.0, 0.0, ALU.mult, ALU.add, d[:, k:k + 1]))
                after(s)
                s = step(v.tensor_tensor(dot2[:, :], d, d, ALU.mult))
                after(s)
                s = step(v.tensor_scalar(cubic[:, :], dot2[:, :], 0.044715, 1.0, ALU.mult, ALU.add))
                after(s)
                v.tensor_tensor(tanh_in[:, slot % 2, :], cubic[:, :], d, ALU.mult).then_inc(tanh_ready, 1)

            def apply(n, slot):
                tile, head, r = slot // PH, slot % PH, slot % RING
                dve.wait_ge(tanh_done, n * SLOTS + (slot + 1))
                s = step(v.scalar_tensor_tensor(out=gated[:, :], in0=tanh[:, slot % 2, :], scalar=1.0,
                                                in1=dot[:, slot % 2, :], op0=ALU.add, op1=ALU.mult))
                after(s)
                s = step(v.tensor_tensor(val[:, :], gated[:, :], weight[:, tile % 2, head * TOPK:(head + 1) * TOPK],
                                         ALU.mult))
                after(s)
                for k in range(TOPK):
                    up = ring[:, r, k, DIM:2 * DIM]
                    if head == 0:
                        last = v.tensor_scalar(acc[:, k, :], up, val[:, k:k + 1], None, ALU.mult)
                    else:
                        last = v.scalar_tensor_tensor(out=acc[:, k, :], in0=up, scalar=val[:, k:k + 1],
                                                      in1=acc[:, k, :], op0=ALU.mult, op1=ALU.add)
                    if k < TOPK - 1:
                        step(last)
                last.then_inc(rows_free, 1)
                if head == PH - 1:
                    finish(n, tile)

            def finish(n, tile):
                dve.wait_ge(rows_free, n * SLOTS + ((tile + 1) * PH + RING))
                s = step(v.tensor_reduce(summed[:, :], acc[:, :, :].rearrange("p k d -> p d k"), AX.X, ALU.add))
                if tile >= 2:
                    dve.wait_ge(out_free[tile % 2], n * 32 + 16)
                else:
                    dve.wait_ge(out_free[tile % 2], n * 32)
                after(s)
                v.tensor_tensor(outt[:, tile % 2, :], summed[:, :], tok[:, tile % 2, DIM:2 * DIM], ALU.add)\
                    .then_inc(out_ready, 1)
                dve.wait_ge(out_ready, n * TILES + (tile + 1))
                dve.sem_inc(tok_free, 1)

            def slots(n, more):
                restart()
                for slot in range(SLOTS):
                    tile, part = slot // PH, slot % PH
                    dots(n, slot)
                    if slot:
                        apply(n, slot - 1)
                    if tile + 1 < TILES:
                        topk_slot(n, tile + 1, part)
                    elif more:
                        topk_slot(n + 1, 0, part)
                    if more:
                        for kind, k in front_at(slot):
                            front(n + 1, kind, k)
                apply(n, SLOTS - 1)

            for stages in FRONT:
                for kind, k in stages:
                    front(0, kind, k)
            for part in range(PH):
                topk_slot(0, 0, part)
            restart()
            with dve.Fori(0, BATCH - 1) as n:
                slots(n, True)
                restart()
            slots(BATCH - 1, False)


def kernel(x, L0_tok_embed_w, L0_tok_embed_b, L0_tok_norm_w, L0_tok_norm_b, L0_tok_dw_w, L0_tok_dw_b,
           L0_tok_ln_w, L0_tok_ln_b, L0_tok_w1, L0_tok_b1, L0_tok_w2, L0_tok_b2, L0_tok_gamma,
           L0_tok_final_ln_w, L0_tok_final_ln_b, L0_attn_Wq, L0_attn_bq, L0_attn_Wk, L0_attn_bk,
           L0_attn_Wv, L0_attn_bv, L0_attn_Wo, L0_attn_bo, L0_ffn_Wq, L0_ffn_bq, L0_ffn_keys,
           L0_ffn_w_down_embed, L0_ffn_w_up_embed):
    import numpy as np
    import concourse.bacc as bacc
    from concourse.bass_utils import run_bass_kernel_spmd

    f = np.asarray
    zeros = np.zeros((LNS - 1 - LAYERS, DIM), np.float32)
    layouts = {
        "x": f(x),
        "embed_w": f(L0_tok_embed_w),
        "conv_b": np.concatenate([f(L0_tok_embed_b)[None], f(L0_tok_dw_b), zeros]).T,
        "dw_w": f(L0_tok_dw_w)[:, :, 0, :].transpose(1, 0, 2).reshape(DIM, LAYERS * TAPS),
        "ln_w": f(L0_tok_ln_w).T,
        "ln_b": f(L0_tok_ln_b).T,
        "w1": f(L0_tok_w1).transpose(2, 0, 1),
        "b1": f(L0_tok_b1).reshape(LAYERS * FBLK, P).T,
        "w2": f(L0_tok_w2).transpose(2, 0, 1).reshape(FBLK, P, LAYERS, DIM).transpose(1, 2, 0, 3)
                          .reshape(P, LAYERS * FBLK, DIM),
        "b2": f(L0_tok_b2).T,
        "gamma": f(L0_tok_gamma).T,
        "wq": f(L0_attn_Wq).T,
        "wkv": np.concatenate([f(L0_attn_Wk), f(L0_attn_Wv)]).T,
        "bkv": np.concatenate([f(L0_attn_bk), f(L0_attn_bv)])[None],
        "wo": f(L0_attn_Wo).T,
        "vecs": np.stack([f(L0_tok_norm_w), f(L0_tok_norm_b), f(L0_tok_final_ln_w), f(L0_tok_final_ln_b),
                          f(L0_attn_bq), f(L0_attn_bo)], axis=1),
        "ffn_wq": f(L0_ffn_Wq).reshape(2 * PH, HALF, DIM).transpose(1, 0, 2),
        "ffn_bq": f(L0_ffn_bq).reshape(2 * PH, HALF).T,
        "keys": f(L0_ffn_keys).reshape(2 * PH, NKEY, HALF).transpose(2, 0, 1),
        "experts": np.concatenate([f(L0_ffn_w_down_embed), f(L0_ffn_w_up_embed)], axis=1),
    }
    arrays = {"in_" + name: np.ascontiguousarray(a) for name, a in layouts.items()}
    nc = bacc.Bacc("TRN2", target_bir_lowering=False, num_devices=1)
    t = {name: nc.dram_tensor("in_" + name, a.shape, mybir.dt.from_np(a.dtype), kind="ExternalInput").ap()
         for name, a in layouts.items()}
    out = nc.dram_tensor("out", (BATCH, SEQ, DIM), F32, kind="ExternalOutput").ap()
    build(nc, t, out)
    r = run_bass_kernel_spmd(nc, [arrays], core_ids=[0])
    return r.results[0]["out"]
```

```python
from contextlib import ExitStack

import concourse.bass as bass
from concourse import mybir

ALU = mybir.AluOpType
ACT = mybir.ActivationFunctionType
AX = mybir.AxisListType
F32 = mybir.dt.float32
U32 = mybir.dt.uint32
BF16 = mybir.dt.bfloat16

P = 128
BATCH, CIN, SEQ = 32, 100, 512
TAPS, PAD = 7, 3
DIM, INTER, LAYERS = 128, 384, 8
FBLK = INTER // P
HEADS, HDIM = 8, 16
PH, HALF, TOPK = 8, 64, 8
NKEY = 128
TILES = SEQ // P
SLOTS = TILES * PH
RING = 4
CHUNK = 4 * NKEY
CHUNKS = PH // 2
TAIL = 7 + 1
CAND = 8 + 4 + 2 * 2 + 4
LNS = LAYERS + 4
LN_FINAL, LN_ATTN, LN_PEER = LAYERS + 1, LAYERS + 2, LAYERS + 3

def front_steps():
    at, steps = 3, {}

    def put(gap, *step):
        nonlocal at
        at += gap
        steps.setdefault(at, []).append(step)

    put(0, "ln", 0)
    put(1, "norm", 0)
    for layer in range(LAYERS):
        put(4, "ln", layer + 1)
        put(1, "norm", layer + 1)
        put(2, "mlp", layer)
    put(2, "ln", LN_FINAL)
    put(1, "norm", LN_FINAL)
    put(2, "ln", LN_ATTN)
    put(1, "norm", LN_ATTN)
    put(2, "qkv", 0)
    put(2, "elu", 0)
    put(1, "kv", 0)
    put(1, "den", 0)
    put(1, "mix", 0)
    put(1, "out", 0)
    put(2, "ln", LN_PEER)
    put(1, "norm", LN_PEER)
    return steps


FRONT = front_steps()
LATE = SLOTS - CHUNKS
assert max(FRONT) < 3 * LATE and max(FRONT) >= 3 * 23
assert min(g for g, f in FRONT.items() if ("out", 0) in f) >= 3 * 22


def topk_parts(slot, more):
    tile, part = slot // PH, slot % PH
    if tile + 1 < TILES:
        c = part // 2
        return [(0, tile + 1, c if part % 2 == 0 else None, c if part % 2 else None, part == 5, part == PH - 1)]
    if more and slot >= LATE:
        c = slot - LATE
        return [(1, 0, c, c, c == 0, c == CHUNKS - 1)]
    return []


def build(nc, t, out):
    with ExitStack() as ctx:
        def sb(name, shape, dt=F32):
            return ctx.enter_context(nc.sbuf_tensor(name, shape, dt))

        def sem(name):
            return ctx.enter_context(nc.semaphore(name))

        def bank(name):
            return ctx.enter_context(nc.psum_tensor(name, [P, 512], F32))

        ident = sb("ident", [P, P])
        center = sb("center", [P, P])
        mean_w = sb("mean_w", [P, P])
        ones = sb("ones", [P, P])
        head_mask = sb("head_mask", [P, P])
        cand_iota = sb("cand_iota", [P, CAND])
        eps = sb("eps", [P, 3])
        emb_w = sb("emb_w", [CIN, TAPS, DIM])
        dw = sb("dw", [P, LAYERS * TAPS, DIM])
        w1 = sb("w1", [P, LAYERS, INTER])
        w2 = sb("w2", [P, LAYERS * FBLK, DIM])
        wq = sb("wq", [P, DIM])
        wkv = sb("wkv", [P, 2 * DIM])
        wo = sb("wo", [P, DIM])
        score_w = sb("score_w", [P, 2 * PH * NKEY])
        score_b = sb("score_b", [3, 2 * PH * NKEY], BF16)
        ones_b = sb("ones_b", [3, P], BF16)
        kv_b = sb("kv_b", [P, 2 * DIM])
        conv_b = sb("conv_b", [P, LNS])
        ln_b1 = sb("ln_b1", [P, LAYERS * FBLK])
        gamma_b2 = sb("gamma_b2", [P, LAYERS])
        vecs = sb("vecs", [P, 6])
        gamma = sb("gamma", [P, LAYERS])
        row_b = sb("row_b", [1, 2 * DIM])

        xin = sb("xin", [CIN, SEQ + 2 * PAD])
        h = sb("h", [P, SEQ + 2 * PAD])
        hin = h[:, PAD:PAD + SEQ]
        square = sb("square", [P, SEQ])
        std = sb("std", [P, TILES])
        rstd = sb("rstd", [P, TILES])
        shift = sb("shift", [P, SEQ])
        xhat = sb("xhat", [P, SEQ])
        hb = sb("hb", [P, SEQ])
        act = sb("act", [P, FBLK, SEQ])
        hf = sb("hf", [P, SEQ])
        h2 = sb("h2", [P, SEQ])
        qc = sb("qc", [P, SEQ])
        q_exp = sb("q_exp", [P, SEQ])
        q_pos = sb("q_pos", [P, SEQ])
        q_elu = sb("q_elu", [P, SEQ])
        kvt = sb("kvt", [P, TILES, 2 * DIM + 1])
        k_exp = sb("k_exp", [P, TILES, DIM])
        k_pos = sb("k_pos", [P, TILES, DIM])
        k_elu = sb("k_elu", [P, TILES, DIM])
        kv_sum = sb("kv_sum", [P, 1])
        kv_m = sb("kv_m", [P, P])
        ks_m = sb("ks_m", [P, HEADS])
        den = sb("den", [P, TILES * HEADS])
        inv_den = sb("inv_den", [P, TILES * HEADS])
        inv_wide = sb("inv_wide", [P, SEQ])
        mixed = sb("mixed", [P, SEQ])

        ring = sb("ring", [P, RING, TOPK, 2 * DIM])
        tok = sb("tok", [P, 2, 2 * DIM])
        expert = sb("expert", [P, 2, PH * TOPK], U32)
        weight = sb("weight", [P, 2, PH * TOPK])
        half = sb("half", [P, 2, 2, 2, TOPK])
        half_u = sb("half_u", [P, 2, 2, TOPK], U32)
        cand = sb("cand", [P, 2, 2, CAND])
        best = sb("best", [P, PH, TOPK])
        pos = sb("pos", [P, 2, TOPK], U32)
        hit = sb("hit", [P, 2 * TOPK, CAND])
        picked = sb("picked", [P, 2 * TOPK, CAND])
        shifted = sb("shifted", [P, PH, TOPK])
        expd = sb("expd", [P, PH, TOPK])
        total = sb("total", [P, PH])
        inv_total = sb("inv_total", [P, PH])
        dot = sb("dot", [P, 2, TOPK])
        dot2 = sb("dot2", [P, TOPK])
        cubic = sb("cubic", [P, TOPK])
        tanh_in = sb("tanh_in", [P, 2, TOPK])
        tanh = sb("tanh", [P, 2, TOPK])
        gated = sb("gated", [P, TOPK])
        val = sb("val", [P, TOPK])
        acc = sb("acc", [P, TOPK, DIM])
        summed = sb("summed", [P, DIM])
        outt = sb("outt", [P, 2, DIM])

        stage = ring[:, :, :, :].rearrange("p r k d -> p (r k d)")
        keys_s = stage[0:HALF, 0:2048].rearrange("p (c e) -> p c e", c=2 * PH)
        fwq_s = stage[0:HALF, 2048:4096].rearrange("p (c e) -> p c e", c=2 * PH)
        emb_s = stage[:, 4096:4096 + CIN * TAPS].rearrange("p (c k) -> p c k", k=TAPS)
        dw_s = stage[:, 4800:4800 + LAYERS * TAPS]
        cb_s = stage[:, 4864:4864 + LNS]
        lnw_s = stage[:, 4880:4880 + LAYERS]
        lnb_s = stage[:, 4888:4888 + LAYERS]
        b1_s = stage[:, 4896:4896 + LAYERS * FBLK]
        b2_s = stage[:, 4920:4920 + LAYERS]
        fbq_s = stage[0:HALF, 4928:4928 + 2 * PH]
        bias_s = stage[0:3, 5120:7168]
        part_s = stage[0:3, 7168:8192].bitcast(BF16)

        bank_a, bank_b = bank("bank_a"), bank("bank_b")
        bank_c = [bank(f"bank_c{i}") for i in range(3)]
        bank_s = [bank(f"bank_s{i}") for i in range(2)]
        bank_t = bank("bank_t")

        (loaded, masks, consts, prep_pe, prep_cp, prep_dve, ready) = map(sem, (
            "loaded", "masks", "consts", "prep_pe", "prep_cp", "prep_dve", "ready"))
        x_loaded = sem("x_loaded")
        centred, squared, shifted_in, varied, rooted, inverted, spread, normed = map(sem, (
            "centred", "squared", "shifted_in", "varied", "rooted", "inverted", "spread", "normed"))
        affine, hidden, gelued, biased, projected, added = map(sem, (
            "affine", "hidden", "gelued", "biased", "projected", "added"))
        qkv_made, clamped, exped, elued, kv_summed, kv_masked, mix_made, mix_done, out_made, h2_done = map(sem, (
            "qkv_made", "clamped", "exped", "elued", "kv_summed", "kv_masked", "mix_made", "mix_done",
            "out_made", "h2_done"))
        den_inverted, den_spread, num_copied = map(sem, ("den_inverted", "den_spread", "num_copied"))
        scored, listed, turned, tok_ready, tok_free = map(sem, (
            "scored", "listed", "turned", "tok_ready", "tok_free"))
        chosen, shift_done, exp_done = map(sem, ("chosen", "shift_done", "exp_done"))
        landed = [sem(f"landed{i}") for i in range(RING)]
        rows_free, tanh_ready, tanh_done = map(sem, ("rows_free", "tanh_ready", "tanh_done"))
        out_ready, out_free = sem("out_ready"), [sem("out_free0"), sem("out_free1")]
        dve_done = sem("dve_done")
        passed = sem("passed")

        block = ctx.enter_context(nc.Block())

        LOADS = [
            (emb_s, t["embed_w"]), (dw_s, t["dw_w"]), (cb_s, t["conv_b"]), (lnw_s, t["ln_w"]),
            (lnb_s, t["ln_b"]), (b1_s, t["b1"]), (b2_s, t["b2"]), (fbq_s, t["ffn_bq"]),
            (keys_s, t["keys"]), (fwq_s, t["ffn_wq"]), (w1[:, :, :], t["w1"]), (w2[:, :, :], t["w2"]),
            (wq[:, :], t["wq"]), (wkv[:, :], t["wkv"]), (wo[:, :], t["wo"]), (vecs[:, :], t["vecs"]),
            (gamma[:, :], t["gamma"]), (row_b[:, :], t["bkv"]),
        ]
        N_LOADS = len(LOADS)

        @block.sync
        def _(sp):
            for dst, src in LOADS:
                sp.dma_start(dst, src).then_inc(loaded, 16)
            sp.wait_ge(masks, 1)
            sp.dma_start(xin[:, PAD:PAD + SEQ], t["x"][0]).then_inc(x_loaded, 16)

            def store(n, tile):
                sp.wait_ge(out_ready, n * TILES + (tile + 1))
                sp.dma_start(out[n, tile * P:(tile + 1) * P, :], outt[:, tile % 2, :])\
                  .then_inc(out_free[tile % 2], 16)

            with sp.Fori(0, BATCH - 1) as n:
                sp.wait_ge(centred, n * LNS + 1)
                sp.dma_start(xin[:, PAD:PAD + SEQ], t["x"][n + 1]).then_inc(x_loaded, 16)
                for tile in range(TILES):
                    store(n, tile)
            for tile in range(TILES):
                store(BATCH - 1, tile)
            for s in out_free:
                sp.wait_ge(s, 16 * BATCH * TILES // 2)

        @block.gpsimd
        def _(pool):
            pool.memset(xin[:, :], 0.0)
            pool.memset(h[:, :], 0.0).then_inc(masks, 1)
            pool.memset(ident[:, :], 0.0)
            pool.memset(mean_w[:, :], 1.0 / DIM)
            pool.memset(eps[:, 0:1], 1e-6)
            pool.memset(eps[:, 1:2], 1e-5)
            pool.memset(eps[:, 2:3], 0.0)
            pool.memset(kvt[:, :, 2 * DIM:2 * DIM + 1], 1.0)
            pool.iota(cand_iota[:, :], pattern=[[1, CAND]], base=0, channel_multiplier=0,
                      allow_small_or_imprecise_dtypes=True)
            pool.memset(head_mask[:, :], 1.0)
            pool.memset(ones[:, :], 1.0).then_inc(masks, 1)
            pool.wait_ge(masks, 2)
            pool.affine_select(out=ident[:, :], in_=ident[:, :], compare_op=ALU.not_equal, fill=1.0,
                               base=0, pattern=[[-1, P]], channel_multiplier=1).then_inc(masks, 1)
            by_head = head_mask[:, :].rearrange("p (g d) -> p g d", d=HDIM)
            pool.affine_select(out=by_head, in_=by_head, compare_op=ALU.is_ge, fill=0.0, base=0,
                               pattern=[[-HDIM, HEADS], [0, HDIM]], channel_multiplier=1).then_inc(masks, 1)
            pool.wait_ge(masks, 4)
            pool.affine_select(out=by_head, in_=by_head, compare_op=ALU.is_ge, fill=0.0, base=HDIM - 1,
                               pattern=[[HDIM, HEADS], [0, HDIM]], channel_multiplier=-1).then_inc(masks, 1)

            def gather(n, slot):
                tile, head = slot // PH, slot % PH
                pool.wait_ge(rows_free, n * SLOTS + (slot + 1))
                pool.wait_ge(chosen, n * (TILES * CHUNKS) + (tile * CHUNKS + head // 2 + 1))
                pool.sem_inc(passed, 1)
                for k in range(TOPK):
                    col = head * TOPK + k
                    pool.indirect_dma_start(
                        ring[:, slot % RING, k, :], None, t["experts"],
                        bass.IndirectOffsetOnAxis(ap=expert[:, tile % 2, col:col + 1], axis=0),
                    ).then_inc(landed[slot % RING], 16)

            pool.wait_ge(ready, 1)
            pool.sem_inc(passed, 1)
            with pool.Fori(0, BATCH) as n:
                for slot in range(SLOTS):
                    gather(n, slot)

        @block.tensor
        def _(pe):
            mm = nc.tensor.matmul
            pe.wait_ge(loaded, 16 * N_LOADS)
            pe.wait_ge(masks, 5)
            pe.wait_ge(consts, 1)
            for k in range(TAPS):
                dst = (bank_a if k < 4 else bank_b)[0:CIN, (k % 4) * DIM:(k % 4 + 1) * DIM]
                last = mm(dst, emb_s[:, :, k], center[:, :], start=True, stop=True)
            last.then_inc(prep_pe, 1)
            for l in range(LAYERS):
                for j in range(FBLK):
                    mm(bank_t[:, l * FBLK + j:l * FBLK + j + 1], w1[:, l, j * P:(j + 1) * P],
                       lnb_s[:, l:l + 1], start=True, stop=True)
            mm(bank_t[:, 32:32 + LNS], center[:, :], cb_s, start=True, stop=True)
            last = mm(bank_t[:, 128:128 + 2 * DIM], ones[0:1, :], row_b[:, :], start=True, stop=True)
            last.then_inc(prep_pe, 1)
            for c in range(CHUNKS):
                if c >= 2:
                    pe.wait_ge(prep_cp, c - 1)
                for i in range(4):
                    hc = 4 * c + i
                    mm(bank_s[c % 2][:, i * NKEY:(i + 1) * NKEY], fwq_s[:, hc, :], keys_s[:, hc, :],
                       start=True, stop=True)
                    last = mm(bank_c[c % 2][0:3, i * NKEY:(i + 1) * NKEY], fbq_s[:, hc:hc + 1].broadcast_to([HALF, 3]),
                              keys_s[:, hc, :], start=True, stop=True)
                last.then_inc(prep_pe, 1)
            pe.wait_ge(ready, 1)

            def front(m, kind, k):
                if kind == "ln":
                    conv = k <= LAYERS
                    if k == 0:
                        pe.wait_ge(x_loaded, (m + 1) * 16)
                    elif k == 1 or k == LN_ATTN:
                        pe.wait_ge(affine, m * 2 + (1 if k == 1 else 2))
                    elif k == LN_PEER:
                        pe.wait_ge(h2_done, m + 1)
                    else:
                        pe.wait_ge(added, m * LAYERS + (k - 1))
                    if conv:
                        src = xin if k == 0 else h
                        for tap in range(TAPS):
                            w = emb_w[:, tap, :] if k == 0 else dw[:, (k - 1) * TAPS + tap, :]
                            last = mm(bank_a[:, :], w, src[:, tap:tap + SEQ], start=(tap == 0),
                                      stop=(tap == TAPS - 1))
                    else:
                        src = {LN_FINAL: hin, LN_ATTN: hf[:, :], LN_PEER: h2[:, :]}[k]
                        last = mm(bank_a[:, :], center[:, :], src, start=True, stop=True)
                    last.then_inc(centred, 1)
                    pe.wait_ge(squared, m * LNS + (k + 1))
                    for i in range(TILES):
                        last = mm(bank_b[:, i:i + 1], square[:, i * P:(i + 1) * P], mean_w[:, 0:1],
                                  start=True, stop=True)
                    last.then_inc(varied, 1)
                elif kind == "norm":
                    pe.wait_ge(inverted, m * LNS + (k + 1))
                    for i in range(TILES):
                        last = mm(bank_b[:, i * P:(i + 1) * P], rstd[:, i:i + 1].broadcast_to([P, P]), ident[:, :],
                                  start=True, stop=True)
                    last.then_inc(spread, 1)
                elif kind == "mlp":
                    pe.wait_ge(normed, m * LNS + (k + 2))
                    for j in range(FBLK):
                        mm(bank_c[j][:, :], w1[:, k, j * P:(j + 1) * P], xhat[:, :], start=True, stop=True)\
                            .then_inc(hidden, 1)
                    for j in range(FBLK):
                        pe.wait_ge(gelued, m * (LAYERS * FBLK) + (k * FBLK + j + 1))
                        last = mm(bank_b[:, :], w2[:, k * FBLK + j, :], act[:, j, :], start=(j == 0),
                                  stop=(j == FBLK - 1))
                    last.then_inc(projected, 1)
                elif kind == "qkv":
                    pe.wait_ge(normed, m * LNS + (LN_ATTN + 1))
                    mm(bank_c[0][:, :], wq[:, :], xhat[:, :], start=True, stop=True).then_inc(qkv_made, 1)
                    for i in range(TILES):
                        last = mm(bank_c[1 + i // 2][:, (i % 2) * 2 * DIM:(i % 2 + 1) * 2 * DIM],
                                  xhat[:, i * P:(i + 1) * P], wkv[:, :], start=True, stop=True)
                    last.then_inc(qkv_made, 1)
                elif kind == "kv":
                    pe.wait_ge(elued, m + 1)
                    for i in range(TILES):
                        last = mm(bank_b[:, 0:DIM + 1], k_elu[:, i, :], kvt[:, i, DIM:2 * DIM + 1],
                                  start=(i == 0), stop=(i == TILES - 1))
                    last.then_inc(kv_summed, 1)
                elif kind == "den":
                    pe.wait_ge(kv_masked, m + 1)
                    for i in range(TILES):
                        last = mm(bank_c[2][:, i * HEADS:(i + 1) * HEADS], q_elu[:, i * P:(i + 1) * P], ks_m[:, :],
                                  start=True, stop=True)
                    last.then_inc(mix_made, 1)
                    mm(bank_c[1][:, :], kv_m[:, :], q_elu[:, :], start=True, stop=True).then_inc(mix_made, 1)
                elif kind == "mix":
                    pe.wait_ge(den_inverted, m + 1)
                    for i in range(TILES):
                        last = mm(bank_c[2][:, i * P:(i + 1) * P],
                                  inv_wide[:, i * P:(i + 1) * P], ident[:, :], start=True, stop=True)
                    last.then_inc(den_spread, 1)
                elif kind == "out":
                    pe.wait_ge(mix_done, m + 1)
                    mm(bank_c[0][:, :], wo[:, :], mixed[:, :], start=True, stop=True).then_inc(out_made, 1)

            def scores(m, tile, c):
                if c == 0 and tile == 0:
                    pe.wait_ge(normed, m * LNS + LNS)
                pe.wait_ge(listed, m * (TILES * CHUNKS) + (tile * CHUNKS + c + 1))
                mm(bank_s[c % 2][:, :], qc[:, tile * P:(tile + 1) * P], score_w[:, c * CHUNK:(c + 1) * CHUNK],
                   start=True, stop=False)
                mm(bank_s[c % 2][:, :], ones_b[:, :], score_b[:, c * CHUNK:(c + 1) * CHUNK],
                   start=False, stop=True).then_inc(scored, 1)

            def turn(m, tile):
                pe.wait_ge(tok_ready, m * TILES + (tile + 1))
                for i, src in enumerate((qc, h2)):
                    last = nc.tensor.transpose(bank_t[:, i * DIM:(i + 1) * DIM],
                                               src[:, tile * P:(tile + 1) * P], ident[:, :])
                last.then_inc(turned, 1)

            def slots(n, more):
                for slot in range(SLOTS):
                    for seg in range(3):
                        if more:
                            for kind, k in FRONT.get(3 * slot + seg, []):
                                front(n + 1, kind, k)
                        if seg == 0:
                            for ahead, tile, c, _, to_turn, _ in topk_parts(slot, more):
                                if c is not None:
                                    scores(n + ahead, tile, c)
                                if to_turn:
                                    turn(n + ahead, tile)

            for seg in sorted(FRONT):
                for kind, k in FRONT[seg]:
                    front(0, kind, k)
            for c in range(CHUNKS):
                scores(0, 0, c)
            turn(0, 0)
            with pe.Fori(0, BATCH - 1) as n:
                slots(n, True)
            slots(BATCH - 1, False)

        @block.scalar
        def _(act_e):
            activate = nc.scalar.activation
            act_e.wait_ge(prep_pe, 1)
            activate(emb_w[:, 0:4, :], bank_a[0:CIN, :].rearrange("p (k d) -> p k d", k=4), ACT.Copy)
            activate(emb_w[:, 4:7, :], bank_b[0:CIN, 0:3 * DIM].rearrange("p (k d) -> p k d", k=3), ACT.Copy)
            act_e.wait_ge(prep_dve, 1)
            activate(conv_b[:, :], bank_t[:, 32:32 + LNS], ACT.Copy)
            activate(kv_b[:, :], bank_t[:, 128:128 + 2 * DIM], ACT.Copy)
            for c in range(CHUNKS):
                act_e.wait_ge(prep_pe, 3 + c)
                activate(score_w[:, c * CHUNK:(c + 1) * CHUNK], bank_s[c % 2][:, :], ACT.Copy)
                activate(bias_s[:, c * CHUNK:(c + 1) * CHUNK], bank_c[c % 2][0:3, :], ACT.Copy)\
                    .then_inc(prep_cp, 1)
            act_e.wait_ge(ready, 1)

            def front(m, kind, k):
                if kind == "ln":
                    nc.scalar.preload_act_table(ACT.Sqrt)
                    act_e.wait_ge(centred, m * LNS + (k + 1))
                    activate(square[:, :], bank_a[:, :], ACT.Square, bias=conv_b[:, k:k + 1]).then_inc(squared, 1)
                    act_e.wait_ge(varied, m * LNS + (k + 1))
                    e = 0 if k <= LN_FINAL else 1
                    activate(std[:, :], bank_b[:, 0:TILES], ACT.Sqrt, bias=eps[:, e:e + 1]).then_inc(rooted, 1)
                    nc.scalar.preload_act_table(ACT.Exp if k == LN_ATTN else ACT.Gelu)
                    activate(shift[:, :], bank_a[:, :], ACT.Identity, bias=conv_b[:, k:k + 1]).then_inc(shifted_in, 1)
                elif kind == "norm":
                    if k in (0, LN_FINAL):
                        act_e.wait_ge(normed, m * LNS + (k + 1))
                        dst, v = (hin, 0) if k == 0 else (hf[:, :], 2)
                        activate(dst, xhat[:, :], ACT.Identity, bias=vecs[:, v + 1:v + 2],
                                 scale=vecs[:, v:v + 1]).then_inc(affine, 1)
                elif kind == "mlp":
                    if k == 0:
                        act_e.wait_ge(affine, m * 2 + 1)
                    else:
                        act_e.wait_ge(added, m * LAYERS + k)
                    activate(hb[:, :], hin, ACT.Identity, bias=gamma_b2[:, k:k + 1]).then_inc(biased, 1)
                    for j in range(FBLK):
                        act_e.wait_ge(hidden, m * (LAYERS * FBLK) + (k * FBLK + j + 1))
                        activate(act[:, j, :], bank_c[j][:, :], ACT.Gelu,
                                 bias=ln_b1[:, k * FBLK + j:k * FBLK + j + 1]).then_inc(gelued, 1)
                elif kind == "elu":
                    act_e.wait_ge(clamped, m * 2 + 1)
                    activate(q_exp[:, :], q_exp[:, :], ACT.Exp).then_inc(exped, 1)
                    act_e.wait_ge(clamped, m * 2 + 2)
                    activate(k_exp[:, :, :], k_exp[:, :, :], ACT.Exp).then_inc(exped, 1)

                elif kind == "mix":
                    act_e.wait_ge(mix_made, m * 2 + 2)
                    activate(q_pos[:, :], bank_c[1][:, :], ACT.Copy).then_inc(num_copied, 1)

            def tanh_slot(n, slot):
                act_e.wait_ge(tanh_ready, n * SLOTS + (slot + 1))
                activate(tanh[:, slot % 2, :], tanh_in[:, slot % 2, :], ACT.Tanh,
                         scale=0.7978845608028654).then_inc(tanh_done, 1)

            def copy_turned(m, tile):
                act_e.wait_ge(turned, m * TILES + (tile + 1))
                act_e.wait_ge(tok_free, m * TILES + (tile + 1))
                activate(tok[:, tile % 2, :], bank_t[:, 0:2 * DIM], ACT.Copy).then_inc(tok_ready, 1)

            def exps(m, tile):
                act_e.wait_ge(shift_done, m * TILES + (tile + 1))
                activate(expd[:, :, :], shifted[:, :, :], ACT.Exp).then_inc(exp_done, 1)

            def slots(n, more):
                for slot in range(SLOTS):
                    for seg in range(3):
                        if more:
                            for kind, k in FRONT.get(3 * slot + seg, []):
                                front(n + 1, kind, k)
                        if seg == 0:
                            tanh_slot(n, slot)
                            for ahead, tile, _, _, to_turn, _ in topk_parts(slot, more):
                                if to_turn:
                                    copy_turned(n + ahead, tile)
                        if seg == 1:
                            for ahead, tile, _, _, _, to_soften in topk_parts(slot, more):
                                if to_soften:
                                    exps(n + ahead, tile)

            for seg in sorted(FRONT):
                for kind, k in FRONT[seg]:
                    front(0, kind, k)
            copy_turned(0, 0)
            exps(0, 0)
            with act_e.Fori(0, BATCH - 1) as n:
                slots(n, True)
            slots(BATCH - 1, False)

        @block.vector
        def _(dve):
            v = nc.vector
            steps = [0]

            def step(ins):
                steps[0] += 1
                ins.then_inc(dve_done, 1)
                return steps[0]

            def after(n):
                dve.wait_ge(dve_done, n)

            def restart():
                dve.wait_ge(dve_done, steps[0])
                dve.sem_clear(dve_done)
                steps[0] = 0

            dve.wait_ge(masks, 5)
            v.tensor_tensor(center[:, :], ident[:, :], mean_w[:, :], ALU.subtract).then_inc(consts, 1)
            dve.wait_ge(loaded, 16 * N_LOADS)
            dve.wait_ge(consts, 1)
            for i in range(LAYERS * TAPS):
                v.tensor_scalar(dw[:, i, :], center[:, :], dw_s[:, i:i + 1], None, ALU.mult)
            v.tensor_tensor(gamma_b2[:, :], gamma[:, :], b2_s, ALU.mult)
            dve.wait_ge(prep_pe, 2)
            v.tensor_tensor(ln_b1[:, :], bank_t[:, 0:LAYERS * FBLK], b1_s, ALU.add).then_inc(prep_dve, 1)
            for l in range(LAYERS):
                last = v.tensor_scalar(w1[:, l, :], w1[:, l, :], lnw_s[:, l:l + 1], None, ALU.mult)
            last.then_inc(prep_dve, 1)
            dve.wait_ge(prep_dve, 2)
            dve.wait_ge(prep_cp, CHUNKS)
            step(v.memset(ones_b[:, :], 1.0))
            for r in range(3):
                after(step(v.tensor_copy(part_s, bias_s)))
                after(step(v.tensor_tensor(bias_s, bias_s, part_s, ALU.subtract)))
                mine = ident[0:3, r:r + 1]
                if r == 0:
                    after(step(v.tensor_scalar(score_b[:, :], part_s, mine, None, ALU.mult)))
                else:
                    after(step(v.scalar_tensor_tensor(out=score_b[:, :], in0=part_s, scalar=mine, in1=score_b[:, :],
                                                      op0=ALU.mult, op1=ALU.add)))
            dve.sem_inc(rows_free, RING)
            dve.sem_inc(listed, 2)
            dve.sem_inc(tok_free, 2)
            dve.sem_inc(tok_ready, 1)
            dve.sem_inc(ready, 1)

            def front(m, kind, k):
                if kind == "ln":
                    dve.wait_ge(rooted, m * LNS + (k + 1))
                    v.reciprocal(rstd[:, :], std[:, :]).then_inc(inverted, 1)
                elif kind == "norm":
                    dst = qc if k == LN_PEER else xhat
                    dve.wait_ge(shifted_in, m * LNS + (k + 1))
                    dve.wait_ge(spread, m * LNS + (k + 1))
                    v.tensor_tensor(dst[:, :], shift[:, :], bank_b[:, :], ALU.mult).then_inc(normed, 1)
                elif kind == "mlp":
                    dve.wait_ge(biased, m * LAYERS + (k + 1))
                    dve.wait_ge(projected, m * LAYERS + (k + 1))
                    v.scalar_tensor_tensor(out=hin, in0=bank_b[:, :], scalar=gamma[:, k:k + 1], in1=hb[:, :],
                                           op0=ALU.mult, op1=ALU.add).then_inc(added, 1)
                elif kind == "qkv":
                    dve.wait_ge(qkv_made, m * 2 + 2)
                    for j in range(2):
                        last = v.tensor_tensor(
                            kvt[:, 2 * j:2 * j + 2, 0:2 * DIM],
                            bank_c[1 + j][:, :].rearrange("p (i d) -> p i d", i=2),
                            kv_b[:, :].unsqueeze(1).broadcast_to([P, 2, 2 * DIM]), ALU.add)
                    biased_at = step(last)
                    q_in = bank_c[0][:, :]
                    v.tensor_scalar(q_exp[:, :], q_in, vecs[:, 4:5], 0.0, ALU.add, ALU.min).then_inc(clamped, 1)
                    after(biased_at)
                    v.tensor_scalar(k_exp[:, :, :], kvt[:, :, 0:DIM], 0.0, None, ALU.min).then_inc(clamped, 1)
                    step(v.tensor_scalar(q_pos[:, :], q_in, vecs[:, 4:5], 0.0, ALU.add, ALU.max))
                    step(v.tensor_scalar(k_pos[:, :, :], kvt[:, :, 0:DIM], 0.0, None, ALU.max))
                elif kind == "elu":
                    dve.wait_ge(exped, m * 2 + 2)
                    after(steps[0])
                    v.tensor_tensor(q_elu[:, :], q_exp[:, :], q_pos[:, :], ALU.add)
                    v.tensor_tensor(k_elu[:, :, :], k_exp[:, :, :], k_pos[:, :, :], ALU.add).then_inc(elued, 1)
                elif kind == "kv":
                    dve.wait_ge(kv_summed, m + 1)
                    s = step(v.tensor_copy(kv_sum[:, :], bank_b[:, DIM:DIM + 1]))
                    v.tensor_tensor(kv_m[:, :], head_mask[:, :], bank_b[:, 0:DIM], ALU.mult)
                    after(s)
                    v.tensor_scalar(ks_m[:, :], head_mask[:, 0:P:HDIM], kv_sum[:, :], None, ALU.mult)\
                        .then_inc(kv_masked, 1)
                elif kind == "den":
                    dve.wait_ge(mix_made, m * 2 + 1)
                    s = step(v.tensor_scalar(den[:, :], bank_c[2][:, 0:TILES * HEADS], 1e-6, None, ALU.add))
                    after(s)
                    s = step(v.reciprocal(inv_den[:, :], den[:, :]))
                    after(s)
                    v.tensor_copy(inv_wide[:, :].rearrange("p (i d) -> p i d", d=HDIM),
                                  inv_den[:, :].unsqueeze(2).broadcast_to([P, TILES * HEADS, HDIM]))\
                        .then_inc(den_inverted, 1)
                elif kind == "mix":
                    dve.wait_ge(num_copied, m + 1)
                    dve.wait_ge(den_spread, m + 1)
                    v.tensor_tensor(mixed[:, :], q_pos[:, :], bank_c[2][:, :], ALU.mult).then_inc(mix_done, 1)
                elif kind == "out":
                    dve.wait_ge(out_made, m + 1)
                    v.scalar_tensor_tensor(out=h2[:, :], in0=bank_c[0][:, :], scalar=vecs[:, 5:6], in1=hf[:, :],
                                           op0=ALU.add, op1=ALU.add).then_inc(h2_done, 1)

            def lists(m, tile, c):
                dve.wait_ge(scored, m * (TILES * CHUNKS) + (tile * CHUNKS + c + 1))
                dve.sem_inc(passed, 1)
                after(steps[0])
                for hd in range(2):
                    for cc in range(2):
                        cols = bank_s[c % 2][:, (2 * hd + cc) * NKEY:(2 * hd + cc + 1) * NKEY]
                        s = step(v.max(half[:, cc, hd, 0, :], cols))
                for hd in range(2):
                    for cc in range(2):
                        cols = bank_s[c % 2][:, (2 * hd + cc) * NKEY:(2 * hd + cc + 1) * NKEY]
                        after(s - 3 + 2 * hd + cc)
                        last = v.max_index(half_u[:, hd, cc, :], half[:, cc, hd, 0, :], cols)
                        if hd == 1 and cc == 1:
                            last.then_inc(listed, 1)

            def pairs(m, tile, c):
                dve.wait_ge(listed, m * (TILES * CHUNKS) + (tile * CHUNKS + c + 3))
                step(v.tensor_scalar(half[:, 0, :, 1, :], half_u[:, :, 0, :], float(NKEY), None, ALU.mult))
                s = step(v.tensor_scalar(half[:, 1, :, 1, :], half_u[:, :, 1, :], 1.0, None, ALU.mult))
                after(s)
                a = half[:, 0, :, :, :].rearrange("p h w k -> p (h w) k")
                b = half[:, 1, :, :, :].rearrange("p h w k -> p (h w) k")
                cd = cand[:, :, :, :].rearrange("p h w k -> p (h w) k")
                step(v.tensor_tensor(cd[:, :, 0:8], a[:, :, 0:1].broadcast_to([P, 4, 8]), b[:, :, 0:8], ALU.add))
                step(v.tensor_tensor(cd[:, :, 8:12], a[:, :, 1:2].broadcast_to([P, 4, 4]), b[:, :, 0:4], ALU.add))
                step(v.tensor_tensor(cd[:, :, 12:16].rearrange("p w (a b) -> p w a b", a=2),
                                     a[:, :, 2:4].unsqueeze(3).broadcast_to([P, 4, 2, 2]),
                                     b[:, :, 0:2].unsqueeze(2).broadcast_to([P, 4, 2, 2]), ALU.add))
                s = step(v.tensor_tensor(cd[:, :, 16:20], a[:, :, 4:8], b[:, :, 0:1].broadcast_to([P, 4, 4]),
                                         ALU.add))
                after(s)
                for hd in range(2):
                    s = step(v.max(best[:, 2 * c + hd, :], cand[:, hd, 0, :]))
                for hd in range(2):
                    after(s - 1 + hd)
                    last = step(v.max_index(pos[:, hd, :], best[:, 2 * c + hd, :], cand[:, hd, 0, :]))
                after(last)
                s = step(v.tensor_tensor(
                    hit[:, :, :], pos[:, :, :].rearrange("p h k -> p (h k)").unsqueeze(2).broadcast_to([P, 16, CAND]),
                    cand_iota[:, :].unsqueeze(1).broadcast_to([P, 16, CAND]), ALU.is_equal))
                after(s)
                s = step(v.tensor_tensor(
                    picked[:, :, :].rearrange("p (h k) c -> p h k c", h=2),
                    hit[:, :, :].rearrange("p (h k) c -> p h k c", h=2),
                    cand[:, :, 1, :].unsqueeze(2).broadcast_to([P, 2, TOPK, CAND]), ALU.mult))
                after(s)
                with nc.allow_low_precision(reason="one whole number under 2^14 and zeros"):
                    v.tensor_reduce(expert[:, tile % 2, 16 * c:16 * c + 16], picked[:, :, :], AX.X, ALU.add)\
                        .then_inc(chosen, 1)

            def soften(m, tile):
                after(steps[0])
                v.tensor_tensor(shifted[:, :, :], best[:, :, :], best[:, :, 0:1].broadcast_to([P, PH, TOPK]),
                                ALU.subtract).then_inc(shift_done, 1)
                dve.wait_ge(exp_done, m * TILES + (tile + 1))
                s = step(v.tensor_reduce(total[:, :], expd[:, :, :], AX.X, ALU.add))
                after(s)
                s = step(v.reciprocal(inv_total[:, :], total[:, :]))
                after(s)
                w = weight[:, tile % 2, :].rearrange("p (h k) -> p h k", h=PH)
                s = step(v.tensor_tensor(w, expd[:, :, :], inv_total[:, :].unsqueeze(2).broadcast_to([P, PH, TOPK]),
                                         ALU.mult))
                after(s)
                step(v.tensor_scalar(weight[:, tile % 2, :], weight[:, tile % 2, :], 0.5, None, ALU.mult))

            def dots(n, slot):
                tile, r = slot // PH, slot % RING
                dve.wait_ge(landed[r], n * (SLOTS // RING * 16 * TOPK) + (slot // RING + 1) * 16 * TOPK)
                if slot % PH == 0:
                    dve.wait_ge(tok_ready, n * TILES + (tile + 2))
                d = dot[:, slot % 2, :]
                for k in range(TOPK):
                    s = step(v.tensor_tensor_reduce(ring[:, r, k, 0:DIM], ring[:, r, k, 0:DIM], tok[:, tile % 2, 0:DIM],
                                                    1.0, 0.0, ALU.mult, ALU.add, d[:, k:k + 1]))
                after(s)
                s = step(v.tensor_tensor(dot2[:, :], d, d, ALU.mult))
                after(s)
                s = step(v.tensor_scalar(cubic[:, :], dot2[:, :], 0.044715, 1.0, ALU.mult, ALU.add))
                after(s)
                v.tensor_tensor(tanh_in[:, slot % 2, :], cubic[:, :], d, ALU.mult).then_inc(tanh_ready, 1)

            def apply(n, slot):
                tile, head, r = slot // PH, slot % PH, slot % RING
                dve.wait_ge(tanh_done, n * SLOTS + (slot + 1))
                s = step(v.scalar_tensor_tensor(out=gated[:, :], in0=tanh[:, slot % 2, :], scalar=1.0,
                                                in1=dot[:, slot % 2, :], op0=ALU.add, op1=ALU.mult))
                after(s)
                s = step(v.tensor_tensor(val[:, :], gated[:, :], weight[:, tile % 2, head * TOPK:(head + 1) * TOPK],
                                         ALU.mult))
                after(s)
                for k in range(TOPK):
                    up = ring[:, r, k, DIM:2 * DIM]
                    if head == 0:
                        last = v.tensor_scalar(acc[:, k, :], up, val[:, k:k + 1], None, ALU.mult)
                    else:
                        last = v.scalar_tensor_tensor(out=acc[:, k, :], in0=up, scalar=val[:, k:k + 1],
                                                      in1=acc[:, k, :], op0=ALU.mult, op1=ALU.add)
                    if k < TOPK - 1:
                        step(last)
                last.then_inc(rows_free, 1)
                if head == PH - 1:
                    finish(n, tile)

            def finish(n, tile):
                dve.wait_ge(rows_free, n * SLOTS + ((tile + 1) * PH + RING))
                s = step(v.tensor_reduce(summed[:, :], acc[:, :, :].rearrange("p k d -> p d k"), AX.X, ALU.add))
                if tile >= 2:
                    dve.wait_ge(out_free[tile % 2], n * 32 + 16)
                else:
                    dve.wait_ge(out_free[tile % 2], n * 32)
                after(s)
                v.tensor_tensor(outt[:, tile % 2, :], summed[:, :], tok[:, tile % 2, DIM:2 * DIM], ALU.add)\
                    .then_inc(out_ready, 1)
                dve.wait_ge(out_ready, n * TILES + (tile + 1))
                dve.sem_inc(tok_free, 1)

            def topk(n, slot, more):
                for ahead, tile, to_list, to_pair, _, to_soften in topk_parts(slot, more):
                    if to_list is not None:
                        lists(n + ahead, tile, to_list)
                    if to_pair is not None:
                        pairs(n + ahead, tile, to_pair)
                    if to_soften:
                        soften(n + ahead, tile)

            def slots(n, more):
                restart()
                for slot in range(SLOTS):
                    for seg in range(3):
                        if seg == 0:
                            dots(n, slot)
                        elif seg == 1 and slot:
                            apply(n, slot - 1)
                        elif seg == 2:
                            topk(n, slot, more)
                        if more:
                            for kind, k in FRONT.get(3 * slot + seg, []):
                                front(n + 1, kind, k)
                apply(n, SLOTS - 1)

            for seg in sorted(FRONT):
                for kind, k in FRONT[seg]:
                    front(0, kind, k)
            for c in range(CHUNKS):
                lists(0, 0, c)
                pairs(0, 0, c)
            soften(0, 0)
            restart()
            with dve.Fori(0, BATCH - 1) as n:
                slots(n, True)
                restart()
            slots(BATCH - 1, False)


def kernel(x, L0_tok_embed_w, L0_tok_embed_b, L0_tok_norm_w, L0_tok_norm_b, L0_tok_dw_w, L0_tok_dw_b,
           L0_tok_ln_w, L0_tok_ln_b, L0_tok_w1, L0_tok_b1, L0_tok_w2, L0_tok_b2, L0_tok_gamma,
           L0_tok_final_ln_w, L0_tok_final_ln_b, L0_attn_Wq, L0_attn_bq, L0_attn_Wk, L0_attn_bk,
           L0_attn_Wv, L0_attn_bv, L0_attn_Wo, L0_attn_bo, L0_ffn_Wq, L0_ffn_bq, L0_ffn_keys,
           L0_ffn_w_down_embed, L0_ffn_w_up_embed):
    import numpy as np
    import concourse.bacc as bacc
    from concourse.bass_utils import run_bass_kernel_spmd

    f = np.asarray
    zeros = np.zeros((LNS - 1 - LAYERS, DIM), np.float32)
    layouts = {
        "x": f(x),
        "embed_w": f(L0_tok_embed_w),
        "conv_b": np.concatenate([f(L0_tok_embed_b)[None], f(L0_tok_dw_b), zeros]).T,
        "dw_w": f(L0_tok_dw_w)[:, :, 0, :].transpose(1, 0, 2).reshape(DIM, LAYERS * TAPS),
        "ln_w": f(L0_tok_ln_w).T,
        "ln_b": f(L0_tok_ln_b).T,
        "w1": f(L0_tok_w1).transpose(2, 0, 1),
        "b1": f(L0_tok_b1).reshape(LAYERS * FBLK, P).T,
        "w2": f(L0_tok_w2).transpose(2, 0, 1).reshape(FBLK, P, LAYERS, DIM).transpose(1, 2, 0, 3)
                          .reshape(P, LAYERS * FBLK, DIM),
        "b2": f(L0_tok_b2).T,
        "gamma": f(L0_tok_gamma).T,
        "wq": f(L0_attn_Wq).T,
        "wkv": np.concatenate([f(L0_attn_Wk), f(L0_attn_Wv)]).T,
        "bkv": np.concatenate([f(L0_attn_bk), f(L0_attn_bv)])[None],
        "wo": f(L0_attn_Wo).T,
        "vecs": np.stack([f(L0_tok_norm_w), f(L0_tok_norm_b), f(L0_tok_final_ln_w), f(L0_tok_final_ln_b),
                          f(L0_attn_bq), f(L0_attn_bo)], axis=1),
        "ffn_wq": f(L0_ffn_Wq).reshape(2 * PH, HALF, DIM).transpose(1, 0, 2),
        "ffn_bq": f(L0_ffn_bq).reshape(2 * PH, HALF).T,
        "keys": f(L0_ffn_keys).reshape(2 * PH, NKEY, HALF).transpose(2, 0, 1),
        "experts": np.concatenate([f(L0_ffn_w_down_embed), f(L0_ffn_w_up_embed)], axis=1),
    }
    arrays = {"in_" + name: np.ascontiguousarray(a) for name, a in layouts.items()}
    nc = bacc.Bacc("TRN2", target_bir_lowering=False, num_devices=1)
    t = {name: nc.dram_tensor("in_" + name, a.shape, mybir.dt.from_np(a.dtype), kind="ExternalInput").ap()
         for name, a in layouts.items()}
    out = nc.dram_tensor("out", (BATCH, SEQ, DIM), F32, kind="ExternalOutput").ap()
    build(nc, t, out)
    r = run_bass_kernel_spmd(nc, [arrays], core_ids=[0])
    return r.results[0]["out"]
```

```python
from contextlib import ExitStack

import concourse.bass as bass
from concourse import mybir

ALU = mybir.AluOpType
ACT = mybir.ActivationFunctionType
AX = mybir.AxisListType
F32 = mybir.dt.float32
U32 = mybir.dt.uint32
BF16 = mybir.dt.bfloat16

P = 128
BATCH, CIN, SEQ = 32, 100, 512
TAPS, PAD = 7, 3
DIM, INTER, LAYERS = 128, 384, 8
FBLK = INTER // P
HEADS, HDIM = 8, 16
PH, HALF, TOPK = 8, 64, 8
NKEY = 128
TILES = SEQ // P
PARTS = [slice(0, SEQ // 2), slice(SEQ // 2, SEQ)]
WIDE = [slice(0, SEQ // 2 + PAD + 1), slice(SEQ // 2 + PAD + 1, SEQ)]
SLOTS = TILES * PH
RING = 8
ON_DVE = TOPK // 2
CHUNK = 4 * NKEY
CHUNKS = PH // 2
CAND = 8 + 4 + 2 * 2 + 4
LNS = LAYERS + 4
LN_FINAL, LN_ATTN, LN_PEER = LAYERS + 1, LAYERS + 2, LAYERS + 3

CYCLES = SLOTS // 2
LN_AT = {0: 0, **{layer + 1: layer + 1 for layer in range(LAYERS)}, LAYERS + 1: LN_FINAL, LAYERS + 3: LN_PEER}
MLP_AT = {layer + 1: layer for layer in range(LAYERS)}
LN_ATTN_AT = LAYERS + 1
ATTN_AT = LAYERS + 2
TURN_AT = 1
assert (TILES - 2) * CHUNKS + TURN_AT < ATTN_AT and (TILES - 1) * CHUNKS - 1 <= ATTN_AT + 1 < (TILES - 1) * CHUNKS


def listed_in(c, more):
    c, ahead = c % CYCLES, c // CYCLES
    if c >= CYCLES - CHUNKS:
        return (ahead + 1, 0, c % CHUNKS) if more else None
    return (ahead, c // CHUNKS + 1, c % CHUNKS) if more or not ahead else None


def paired_in(c, more):
    return (0, 0, CHUNKS - 1) if c == 0 else listed_in(c - 1, more)


def build(nc, t, out):
    with ExitStack() as ctx:
        def sb(name, shape, dt=F32):
            return ctx.enter_context(nc.sbuf_tensor(name, shape, dt))

        def sem(name):
            return ctx.enter_context(nc.semaphore(name))

        def bank(name):
            return ctx.enter_context(nc.psum_tensor(name, [P, 512], F32))

        ident = sb("ident", [P, P])
        center = sb("center", [P, P])
        mean_w = sb("mean_w", [P, P])
        ones = sb("ones", [P, P])
        head_mask = sb("head_mask", [P, P])
        cand_iota = sb("cand_iota", [P, CAND])
        eps = sb("eps", [P, 3])
        emb_w = sb("emb_w", [CIN, TAPS, DIM])
        dw = sb("dw", [P, LAYERS * TAPS, DIM])
        w1 = sb("w1", [P, LAYERS, INTER])
        w2 = sb("w2", [P, LAYERS * FBLK, DIM])
        wq = sb("wq", [P, DIM])
        wkv = sb("wkv", [P, 2 * DIM])
        wo = sb("wo", [P, DIM])
        score_w = sb("score_w", [P, 2 * PH * NKEY])
        score_b = sb("score_b", [3, 2 * PH * NKEY], BF16)
        ones_b = sb("ones_b", [3, P], BF16)
        kv_b = sb("kv_b", [P, 2 * DIM])
        conv_b = sb("conv_b", [P, LNS])
        ln_b1 = sb("ln_b1", [P, LAYERS * FBLK])
        gamma_b2 = sb("gamma_b2", [P, LAYERS])
        vecs = sb("vecs", [P, 6])
        gamma = sb("gamma", [P, LAYERS])
        row_b = sb("row_b", [1, 2 * DIM])

        xin = sb("xin", [CIN, SEQ + 2 * PAD])
        h = sb("h", [P, SEQ + 2 * PAD])
        hin = h[:, PAD:PAD + SEQ]
        square = sb("square", [P, SEQ])
        std = sb("std", [P, TILES])
        rstd = sb("rstd", [P, TILES])
        shift = sb("shift", [P, SEQ])
        xhat = sb("xhat", [P, SEQ])
        hb = sb("hb", [P, SEQ])
        act = sb("act", [P, FBLK, SEQ])
        hf = sb("hf", [P, SEQ])
        h2 = sb("h2", [P, SEQ])
        qc = sb("qc", [P, SEQ])
        q_exp = sb("q_exp", [P, SEQ])
        q_pos = sb("q_pos", [P, SEQ])
        q_elu = sb("q_elu", [P, SEQ])
        kvt = sb("kvt", [P, TILES, 2 * DIM + 1])
        k_exp = sb("k_exp", [P, TILES, DIM])
        k_pos = sb("k_pos", [P, TILES, DIM])
        k_elu = sb("k_elu", [P, TILES, DIM])
        kv_sum = sb("kv_sum", [P, 1])
        kv_m = sb("kv_m", [P, P])
        ks_m = sb("ks_m", [P, HEADS])
        den = sb("den", [P, TILES * HEADS])
        inv_den = sb("inv_den", [P, TILES * HEADS])
        inv_wide = sb("inv_wide", [P, SEQ])
        mixed = sb("mixed", [P, SEQ])

        ring = sb("ring", [P, RING, TOPK, 2 * DIM])
        tok = sb("tok", [P, 2, 2 * DIM])
        expert = sb("expert", [P, 2, PH * TOPK], U32)
        weight = sb("weight", [P, 2, PH * TOPK])
        half = sb("half", [P, 2, 2, 2, TOPK])
        half_u = sb("half_u", [P, 2, 2, TOPK], U32)
        cand = sb("cand", [P, 2, 2, CAND])
        best = sb("best", [P, PH, TOPK])
        pos = sb("pos", [P, 2, TOPK], U32)
        hit = sb("hit", [P, 2 * TOPK, CAND])
        picked = sb("picked", [P, 2 * TOPK, CAND])
        shifted = sb("shifted", [P, PH, TOPK])
        expd = sb("expd", [P, PH, TOPK])
        total = sb("total", [P, PH])
        inv_total = sb("inv_total", [P, PH])
        dot = sb("dot", [P, 2, 2 * TOPK])
        dot2 = sb("dot2", [P, 2 * TOPK])
        cubic = sb("cubic", [P, 2 * TOPK])
        tanh_in = sb("tanh_in", [P, 2, 2 * TOPK])
        tanh = sb("tanh", [P, 2, 2 * TOPK])
        gated = sb("gated", [P, 2 * TOPK])
        val = sb("val", [P, 2, 2 * TOPK])
        acc = sb("acc", [P, ON_DVE, DIM])
        summed_d = sb("summed_d", [P, DIM])
        summed_t = sb("summed_t", [P, DIM])
        summed = sb("summed", [P, DIM])
        outt = sb("outt", [P, 2, DIM])

        stage = ring[:, :, :, :].rearrange("p r k d -> p (r k d)")
        keys_s = stage[0:HALF, 0:2048].rearrange("p (c e) -> p c e", c=2 * PH)
        fwq_s = stage[0:HALF, 2048:4096].rearrange("p (c e) -> p c e", c=2 * PH)
        emb_s = stage[:, 4096:4096 + CIN * TAPS].rearrange("p (c k) -> p c k", k=TAPS)
        dw_s = stage[:, 4800:4800 + LAYERS * TAPS]
        cb_s = stage[:, 4864:4864 + LNS]
        lnw_s = stage[:, 4880:4880 + LAYERS]
        lnb_s = stage[:, 4888:4888 + LAYERS]
        b1_s = stage[:, 4896:4896 + LAYERS * FBLK]
        b2_s = stage[:, 4920:4920 + LAYERS]
        fbq_s = stage[0:HALF, 4928:4928 + 2 * PH]
        bias_s = stage[0:3, 5120:7168]
        part_s = stage[0:3, 7168:8192].bitcast(BF16)

        bank_a, bank_b = bank("bank_a"), bank("bank_b")
        bank_c = [bank(f"bank_c{i}") for i in range(3)]
        bank_s = [bank(f"bank_s{i}") for i in range(2)]
        centred_bank, spread_bank, product_bank = (bank_a, bank_c[2]), (bank_b, bank_c[1]), (bank_b, bank_c[0])
        bank_u = bank("bank_u")

        first_loaded, loaded, masks, consts = map(sem, ("first_loaded", "loaded", "masks", "consts"))
        emb_made, emb_copied, ln_b_made, ln_b_read, kv_b_copied = map(sem, (
            "emb_made", "emb_copied", "ln_b_made", "ln_b_read", "kv_b_copied"))
        conv_ready, w1_ready, score_w_made, score_w_copied, score_b_ready = map(sem, (
            "conv_ready", "w1_ready", "score_w_made", "score_w_copied", "score_b_ready"))
        x_loaded = sem("x_loaded")
        centred, squared, shifted_in, varied, rooted, inverted, spread, normed = map(sem, (
            "centred", "squared", "shifted_in", "varied", "rooted", "inverted", "spread", "normed"))
        affine, hidden, gelued, biased, projected, added = map(sem, (
            "affine", "hidden", "gelued", "biased", "projected", "added"))
        qkv_made, clamped, exped, elued, kv_summed, kv_masked, mix_made, mix_done, out_made, h2_done = map(sem, (
            "qkv_made", "clamped", "exped", "elued", "kv_summed", "kv_masked", "mix_made", "mix_done",
            "out_made", "h2_done"))
        den_inverted, den_spread, num_copied = map(sem, ("den_inverted", "den_spread", "num_copied"))
        scored, listed, turned, tok_ready, tok_free = map(sem, (
            "scored", "listed", "turned", "tok_ready", "tok_free"))
        chosen, shift_done, exp_done = map(sem, ("chosen", "shift_done", "exp_done"))
        landed = [sem(f"landed{i}") for i in range(RING)]
        applied, row_summed = sem("applied"), sem("row_summed")
        tanh_ready, tanh_done, val_ready = map(sem, ("tanh_ready", "tanh_done", "val_ready"))
        scaled = sem("scaled")
        sum_read = sem("sum_read")
        out_ready, out_free = sem("out_ready"), [sem("out_free0"), sem("out_free1")]
        dve_done = sem("dve_done")
        passed = sem("passed")

        block = ctx.enter_context(nc.Block())

        FIRST_LOADS = [
            (emb_s, t["embed_w"]), (cb_s, t["conv_b"]), (dw_s, t["dw_w"]), (vecs[:, :], t["vecs"]),
            (gamma[:, :], t["gamma"]), (b2_s, t["b2"]),
        ]
        LOADS = [
            (lnw_s, t["ln_w"]), (lnb_s, t["ln_b"]), (b1_s, t["b1"]), (w1[:, :, :], t["w1"]), (row_b[:, :], t["bkv"]),
            (w2[:, :, :], t["w2"]), (fbq_s, t["ffn_bq"]), (keys_s, t["keys"]), (fwq_s, t["ffn_wq"]),
            (wq[:, :], t["wq"]), (wkv[:, :], t["wkv"]), (wo[:, :], t["wo"]),
        ]

        @block.sync
        def _(sp):
            for dst, src in FIRST_LOADS:
                sp.dma_start(dst, src).then_inc(first_loaded, 16)
            sp.dma_start(xin[:, PAD:PAD + SEQ], t["x"][0]).then_inc(x_loaded, 16)
            for dst, src in LOADS:
                sp.dma_start(dst, src).then_inc(loaded, 16)

            def store(n, tile):
                sp.wait_ge(out_ready, n * TILES + (tile + 1))
                sp.dma_start(out[n, tile * P:(tile + 1) * P, :], outt[:, tile % 2, :])\
                  .then_inc(out_free[tile % 2], 16)

            def load(m):
                sp.wait_ge(centred, (m - 1) * 2 * LNS + 2)
                sp.dma_start(xin[:, PAD:PAD + SEQ], t["x"][m]).then_inc(x_loaded, 16)

            def stores(n, more):
                for tile in range(TILES):
                    if more and tile == TILES - 1:
                        load(n + 2)
                    store(n, tile)

            load(1)
            with sp.Fori(0, BATCH - 2) as n:
                stores(n, True)
            stores(BATCH - 2, False)
            stores(BATCH - 1, False)
            for s in out_free:
                sp.wait_ge(s, 16 * BATCH * TILES // 2)

        @block.gpsimd
        def _(pool):
            pool.memset(ident[:, :], 0.0).then_inc(masks, 1)
            pool.memset(mean_w[:, :], 1.0 / DIM)
            for padded in (xin, h):
                pool.memset(padded[:, 0:PAD], 0.0)
                pool.memset(padded[:, PAD + SEQ:SEQ + 2 * PAD], 0.0)
            pool.memset(eps[:, 0:1], 1e-6)
            pool.memset(eps[:, 1:2], 1e-5)
            pool.memset(eps[:, 2:3], 0.0)
            pool.memset(kvt[:, :, 2 * DIM:2 * DIM + 1], 1.0)
            pool.iota(cand_iota[:, :], pattern=[[1, CAND]], base=0, channel_multiplier=0,
                      allow_small_or_imprecise_dtypes=True)
            pool.memset(head_mask[:, :], 1.0)
            pool.memset(ones[:, :], 1.0).then_inc(masks, 1)
            pool.wait_ge(masks, 2)
            pool.affine_select(out=ident[:, :], in_=ident[:, :], compare_op=ALU.not_equal, fill=1.0,
                               base=0, pattern=[[-1, P]], channel_multiplier=1).then_inc(masks, 1)
            by_head = head_mask[:, :].rearrange("p (g d) -> p g d", d=HDIM)
            pool.affine_select(out=by_head, in_=by_head, compare_op=ALU.is_ge, fill=0.0, base=0,
                               pattern=[[-HDIM, HEADS], [0, HDIM]], channel_multiplier=1).then_inc(masks, 1)
            pool.wait_ge(masks, 4)
            pool.affine_select(out=by_head, in_=by_head, compare_op=ALU.is_ge, fill=0.0, base=HDIM - 1,
                               pattern=[[HDIM, HEADS], [0, HDIM]], channel_multiplier=-1).then_inc(masks, 1)

            def gather(n, slot):
                tile, head = slot // PH, slot % PH
                pool.wait_ge(applied, n * SLOTS + (slot + 1))
                pool.wait_ge(row_summed, n * SLOTS + (slot + 1))
                pool.wait_ge(chosen, n * (TILES * CHUNKS) + (tile * CHUNKS + head // 2 + 1))
                pool.sem_inc(passed, 1)
                for k in range(TOPK):
                    col = head * TOPK + k
                    pool.indirect_dma_start(
                        ring[:, slot % RING, k, :], None, t["experts"],
                        bass.IndirectOffsetOnAxis(ap=expert[:, tile % 2, col:col + 1], axis=0),
                    ).then_inc(landed[slot % RING], 16)

            with pool.Fori(0, BATCH) as n:
                for slot in range(SLOTS):
                    gather(n, slot)

        @block.tensor
        def _(pe):
            mm = nc.tensor.matmul

            def make_embedding():
                pe.wait_ge(first_loaded, 16 * len(FIRST_LOADS))
                pe.wait_ge(masks, 5)
                pe.wait_ge(consts, 1)
                for k in range(TAPS):
                    dst = (bank_a if k < 4 else bank_b)[0:CIN, (k % 4) * DIM:(k % 4 + 1) * DIM]
                    mm(dst, emb_s[:, :, k], center[:, :], start=True, stop=True)
                mm(bank_u[:, 0:LNS], center[:, :], cb_s, start=True, stop=True).then_inc(emb_made, 1)
                pe.wait_ge(emb_copied, 1)

            def make_ln_b(layer):
                if layer == 0:
                    pe.wait_ge(loaded, 16 * len(LOADS))
                elif layer == 1:
                    pe.wait_ge(kv_b_copied, 1)
                else:
                    pe.wait_ge(ln_b_read, layer)
                for j in range(FBLK):
                    last = mm(bank_u[:, layer * FBLK + j:layer * FBLK + j + 1], w1[:, layer, j * P:(j + 1) * P],
                              lnb_s[:, layer:layer + 1], start=True, stop=True)
                if layer == 0:
                    last = mm(bank_u[:, 128:128 + 2 * DIM], ones[0:1, :], row_b[:, :], start=True, stop=True)
                last.then_inc(ln_b_made, 1)

            def make_score_w(c):
                if c:
                    pe.wait_ge(score_w_copied, c)
                for i in range(4):
                    hc = 4 * c + i
                    mm(bank_s[0][:, i * NKEY:(i + 1) * NKEY], fwq_s[:, hc, :], keys_s[:, hc, :],
                       start=True, stop=True)
                    last = mm(bank_s[1][0:3, i * NKEY:(i + 1) * NKEY], fbq_s[:, hc:hc + 1].broadcast_to([HALF, 3]),
                              keys_s[:, hc, :], start=True, stop=True)
                last.then_inc(score_w_made, 1)

            def centre(m, k):
                if k == 0:
                    pe.wait_ge(x_loaded, (m + 1) * 16)
                elif k == 1 or k == LN_ATTN:
                    pe.wait_ge(affine, m * 2 + (1 if k == 1 else 2))
                elif k == LN_PEER:
                    pe.wait_ge(h2_done, m + 1)
                for i, p in enumerate(PARTS):
                    if 2 <= k <= LN_FINAL:
                        pe.wait_ge(added, m * 2 * LAYERS + (2 * (k - 2) + i + 1))
                    dst = centred_bank[i][:, 0:SEQ // 2]
                    if k <= LAYERS:
                        src = xin if k == 0 else h
                        for tap in range(TAPS):
                            w = emb_w[:, tap, :] if k == 0 else dw[:, (k - 1) * TAPS + tap, :]
                            last = mm(dst, w, src[:, tap + p.start:tap + p.stop], start=(tap == 0),
                                      stop=(tap == TAPS - 1))
                    else:
                        src = {LN_FINAL: hin, LN_ATTN: hf, LN_PEER: h2}[k]
                        last = mm(dst, center[:, :], src[:, p], start=True, stop=True)
                    last.then_inc(centred, 1)

            def variance(m, k):
                for i in range(TILES):
                    if i % (TILES // 2) == 0:
                        pe.wait_ge(squared, m * 2 * LNS + (2 * k + i // (TILES // 2) + 1))
                    last = mm(bank_b[:, i:i + 1], square[:, i * P:(i + 1) * P], mean_w[:, 0:1],
                              start=True, stop=True)
                last.then_inc(varied, 1)

            def spread_std(m, k):
                pe.wait_ge(inverted, m * LNS + (k + 1))
                for i in range(TILES):
                    col = i % (TILES // 2) * P
                    last = mm(spread_bank[i // (TILES // 2)][:, col:col + P], rstd[:, i:i + 1].broadcast_to([P, P]),
                              ident[:, :], start=True, stop=True)
                    if i % (TILES // 2):
                        last.then_inc(spread, 1)

            def mlp(m, k):
                for j in range(FBLK):
                    for i, p in enumerate(PARTS):
                        if j == 0:
                            pe.wait_ge(normed, m * 2 * LNS + (2 * (k + 1) + i + 1))
                        last = mm(bank_c[j][:, p], w1[:, k, j * P:(j + 1) * P], xhat[:, p], start=True, stop=True)
                    last.then_inc(hidden, 1)
                for j, i in ((0, 0), (0, 1), (1, 0), (2, 0), (1, 1), (2, 1)):
                    if i == 0:
                        pe.wait_ge(gelued, m * (LAYERS * FBLK) + (k * FBLK + j + 1))
                    w = WIDE[i]
                    last = mm(product_bank[i][:, 0:w.stop - w.start], w2[:, k * FBLK + j, :], act[:, j, w],
                              start=(j == 0), stop=(j == FBLK - 1))
                    if j == FBLK - 1:
                        last.then_inc(projected, 1)

            def qkv(m):
                pe.wait_ge(normed, m * 2 * LNS + 2 * (LN_ATTN + 1))
                mm(bank_c[0][:, :], wq[:, :], xhat[:, :], start=True, stop=True)
                for i in range(TILES):
                    last = mm(bank_c[1 + i // 2][:, (i % 2) * 2 * DIM:(i % 2 + 1) * 2 * DIM],
                              xhat[:, i * P:(i + 1) * P], wkv[:, :], start=True, stop=True)
                last.then_inc(qkv_made, 1)

            def kv(m):
                pe.wait_ge(elued, m + 1)
                for i in range(TILES):
                    last = mm(bank_b[:, 0:DIM + 1], k_elu[:, i, :], kvt[:, i, DIM:2 * DIM + 1],
                              start=(i == 0), stop=(i == TILES - 1))
                last.then_inc(kv_summed, 1)

            def mix(m):
                pe.wait_ge(kv_masked, m + 1)
                for i in range(TILES):
                    last = mm(bank_c[2][:, i * HEADS:(i + 1) * HEADS], q_elu[:, i * P:(i + 1) * P], ks_m[:, :],
                              start=True, stop=True)
                last.then_inc(mix_made, 1)
                mm(bank_c[1][:, :], kv_m[:, :], q_elu[:, :], start=True, stop=True).then_inc(mix_made, 1)

            def spread_den(m):
                pe.wait_ge(den_inverted, m + 1)
                for i in range(TILES):
                    last = mm(bank_c[2][:, i * P:(i + 1) * P],
                              inv_wide[:, i * P:(i + 1) * P], ident[:, :], start=True, stop=True)
                last.then_inc(den_spread, 1)

            def attn_out(m):
                pe.wait_ge(mix_done, m + 1)
                mm(bank_c[0][:, :], wo[:, :], mixed[:, :], start=True, stop=True).then_inc(out_made, 1)

            def scores(m, tile, c):
                if c == 0 and tile == 0:
                    pe.wait_ge(normed, m * 2 * LNS + 2 * LNS)
                pe.wait_ge(listed, m * (TILES * CHUNKS) + (tile * CHUNKS + c + 1))
                if c == 2:
                    pe.wait_ge(tok_ready, m * TILES + (tile + 2))
                mm(bank_s[c % 2][:, :], qc[:, tile * P:(tile + 1) * P], score_w[:, c * CHUNK:(c + 1) * CHUNK],
                   start=True, stop=False)
                mm(bank_s[c % 2][:, :], ones_b[:, :], score_b[:, c * CHUNK:(c + 1) * CHUNK],
                   start=False, stop=True).then_inc(scored, 1)

            def turn(m, tile):
                pe.wait_ge(listed, m * (TILES * CHUNKS) + (tile * CHUNKS + 3))
                for i, src in enumerate((qc, h2)):
                    last = nc.tensor.transpose(bank_s[0][:, i * DIM:(i + 1) * DIM],
                                               src[:, tile * P:(tile + 1) * P], ident[:, :])
                last.then_inc(turned, 1)

            def sum_rows(n, slot):
                tile, head = slot // PH, slot % PH
                if head == 0:
                    pe.wait_ge(sum_read, n * TILES + (tile + 1))
                pe.wait_ge(scaled, n * SLOTS + (slot + 4))
                mm(bank_u[:, :].rearrange("p (k d) -> p k d", d=DIM), ident[:, :],
                   ring[:, slot % RING, ON_DVE:TOPK, DIM:2 * DIM], start=(head == 0), stop=(head == PH - 1))\
                    .then_inc(row_summed, 1)

            def cycle(n, c, more):
                m = n + 1
                k = LN_AT.get(c) if more else None
                late = more and c in (ATTN_AT, ATTN_AT + 1)
                if late:
                    sum_rows(n, 2 * c - 2)
                if late and c == ATTN_AT + 1:
                    sum_rows(n, 2 * c - 1)
                if more and c == ATTN_AT:
                    qkv(m)
                if k is not None:
                    centre(m, k)
                if c and not late:
                    sum_rows(n, 2 * c - 2)
                if c % CHUNKS == TURN_AT and listed_in(c, more):
                    ahead, tile, _ = listed_in(c, more)
                    turn(n + ahead, tile)
                if k is not None:
                    variance(m, k)
                    spread_std(m, k)
                if more and c == ATTN_AT:
                    kv(m)
                if c and not (late and c == ATTN_AT + 1):
                    sum_rows(n, 2 * c - 1)
                if more and c in MLP_AT:
                    mlp(m, MLP_AT[c])
                if more and c == LN_ATTN_AT:
                    centre(m, LN_ATTN)
                    variance(m, LN_ATTN)
                    spread_std(m, LN_ATTN)
                if more and c == ATTN_AT:
                    mix(m)
                    spread_den(m)
                    attn_out(m)
                if listed_in(c + 1, more):
                    ahead, tile, chunk = listed_in(c + 1, more)
                    scores(n + ahead, tile, chunk)

            def cycles(n, more):
                for c in range(CYCLES):
                    cycle(n, c, more)
                sum_rows(n, SLOTS - 2)
                sum_rows(n, SLOTS - 1)

            make_embedding()
            for k in range(LNS):
                if 1 <= k <= LAYERS:
                    pe.wait_ge(conv_ready, k)
                centre(0, k)
                if 1 <= k <= CHUNKS:
                    make_score_w(k - 1)
                variance(0, k)
                spread_std(0, k)
                if k < LAYERS:
                    make_ln_b(k)
                if 1 <= k <= LAYERS:
                    pe.wait_ge(w1_ready, k)
                    mlp(0, k - 1)
                if k == LN_ATTN:
                    qkv(0)
                    kv(0)
                    mix(0)
                    spread_den(0)
                    attn_out(0)
            pe.wait_ge(score_w_copied, CHUNKS)
            pe.wait_ge(score_b_ready, 1)
            scores(0, 0, 0)
            scores(0, 0, 1)
            turn(0, 0)
            scores(0, 0, 2)
            scores(0, 0, 3)
            scores(0, 1, 0)
            with pe.Fori(0, BATCH - 1) as n:
                cycles(n, True)
            cycles(BATCH - 1, False)

        @block.scalar
        def _(act_e):
            activate = nc.scalar.activation

            def copy_embedding():
                act_e.wait_ge(emb_made, 1)
                activate(emb_w[:, 0:4, :], bank_a[0:CIN, :].rearrange("p (k d) -> p k d", k=4), ACT.Copy)
                activate(emb_w[:, 4:7, :], bank_b[0:CIN, 0:3 * DIM].rearrange("p (k d) -> p k d", k=3), ACT.Copy)
                activate(conv_b[:, :], bank_u[:, 0:LNS], ACT.Copy).then_inc(emb_copied, 1)

            def copy_kv_b():
                act_e.wait_ge(ln_b_read, 1)
                activate(kv_b[:, :], bank_u[:, 128:128 + 2 * DIM], ACT.Copy).then_inc(kv_b_copied, 1)

            def copy_score_w(c):
                act_e.wait_ge(score_w_made, c + 1)
                activate(score_w[:, c * CHUNK:(c + 1) * CHUNK], bank_s[0][:, :], ACT.Copy)
                activate(bias_s[:, c * CHUNK:(c + 1) * CHUNK], bank_s[1][0:3, :], ACT.Copy)\
                    .then_inc(score_w_copied, 1)

            def squares(m, k):
                for i, p in enumerate(PARTS):
                    act_e.wait_ge(centred, m * 2 * LNS + (2 * k + i + 1))
                    activate(square[:, p], centred_bank[i][:, 0:SEQ // 2], ACT.Square, bias=conv_b[:, k:k + 1])\
                        .then_inc(squared, 1)

            def roots(m, k):
                act_e.wait_ge(varied, m * LNS + (k + 1))
                e = 0 if k <= LN_FINAL else 1
                activate(std[:, :], bank_b[:, 0:TILES], ACT.Sqrt, bias=eps[:, e:e + 1]).then_inc(rooted, 1)
                for i, p in enumerate(PARTS):
                    activate(shift[:, p], centred_bank[i][:, 0:SEQ // 2], ACT.Identity, bias=conv_b[:, k:k + 1])\
                        .then_inc(shifted_in, 1)
                nc.scalar.preload_act_table(ACT.Exp if k == LN_ATTN else ACT.Gelu)

            def stats(m, k):
                nc.scalar.preload_act_table(ACT.Sqrt)
                squares(m, k)
                roots(m, k)

            def affine_of(m, k):
                act_e.wait_ge(normed, m * 2 * LNS + 2 * (k + 1))
                dst, v = (hin, 0) if k == 0 else (hf[:, :], 2)
                activate(dst, xhat[:, :], ACT.Identity, bias=vecs[:, v + 1:v + 2],
                         scale=vecs[:, v:v + 1]).then_inc(affine, 1)

            def bias_h(m, k):
                if k == 0:
                    act_e.wait_ge(affine, m * 2 + 1)
                else:
                    act_e.wait_ge(added, m * 2 * LAYERS + 2 * k)
                activate(hb[:, :], hin, ACT.Identity, bias=gamma_b2[:, k:k + 1]).then_inc(biased, 1)

            def gelus(m, k):
                for j in range(FBLK):
                    act_e.wait_ge(hidden, m * (LAYERS * FBLK) + (k * FBLK + j + 1))
                    activate(act[:, j, :], bank_c[j][:, :], ACT.Gelu,
                             bias=ln_b1[:, k * FBLK + j:k * FBLK + j + 1]).then_inc(gelued, 1)

            def qk_exps(m):
                act_e.wait_ge(clamped, m * 2 + 1)
                activate(q_exp[:, :], q_exp[:, :], ACT.Exp).then_inc(exped, 1)
                act_e.wait_ge(clamped, m * 2 + 2)
                activate(k_exp[:, :, :], k_exp[:, :, :], ACT.Exp).then_inc(exped, 1)

            def copy_num(m):
                act_e.wait_ge(mix_made, m * 2 + 2)
                activate(q_pos[:, :], bank_c[1][:, :], ACT.Copy).then_inc(num_copied, 1)

            def tanh_pair(n, pair):
                act_e.wait_ge(tanh_ready, n * (SLOTS // 2) + (pair + 1))
                activate(tanh[:, pair % 2, :], tanh_in[:, pair % 2, :], ACT.Tanh,
                         scale=0.7978845608028654).then_inc(tanh_done, 1)

            def scale_rows(n, slot):
                pair = slot // 2
                act_e.wait_ge(val_ready, n * (SLOTS // 2) + (pair + 1))
                for k in range(ON_DVE, TOPK):
                    up = ring[:, slot % RING, k, DIM:2 * DIM]
                    col = slot % 2 * TOPK + k
                    last = activate(up, up, ACT.Copy, scale=val[:, pair % 2, col:col + 1])
                last.then_inc(scaled, 1)

            def copy_turned(m, tile):
                act_e.wait_ge(turned, m * TILES + (tile + 1))
                act_e.wait_ge(tok_free, m * TILES + (tile + 1))
                activate(tok[:, tile % 2, :], bank_s[0][:, 0:2 * DIM], ACT.Copy).then_inc(tok_ready, 1)

            def exps(m, tile):
                act_e.wait_ge(shift_done, m * TILES + (tile + 1))
                activate(expd[:, :, :], shifted[:, :, :], ACT.Exp).then_inc(exp_done, 1)

            def cycle(n, c, more):
                m = n + 1
                k = LN_AT.get(c) if more else None
                if more and c in MLP_AT:
                    bias_h(m, MLP_AT[c])
                if c:
                    scale_rows(n, 2 * c - 1)
                if more and c == ATTN_AT:
                    qk_exps(m)
                tanh_pair(n, c)
                if k is not None and c % CHUNKS:
                    nc.scalar.preload_act_table(ACT.Sqrt)
                if k is not None:
                    squares(m, k)
                if c % CHUNKS == 0:
                    exps(n, c // CHUNKS)
                    if k is not None:
                        nc.scalar.preload_act_table(ACT.Sqrt)
                if k is not None:
                    roots(m, k)
                if c % CHUNKS == TURN_AT and listed_in(c, more):
                    ahead, tile, _ = listed_in(c, more)
                    copy_turned(n + ahead, tile)
                scale_rows(n, 2 * c)
                if k in (0, LN_FINAL):
                    affine_of(m, k)
                if more and c in MLP_AT:
                    gelus(m, MLP_AT[c])
                if more and c == LN_ATTN_AT:
                    stats(m, LN_ATTN)
                if more and c == ATTN_AT:
                    copy_num(m)

            def cycles(n, more):
                for c in range(CYCLES):
                    cycle(n, c, more)
                scale_rows(n, SLOTS - 1)

            copy_embedding()
            for k in range(LNS):
                stats(0, k)
                if k in (0, LN_FINAL):
                    affine_of(0, k)
                if k == 0:
                    copy_kv_b()
                if 1 <= k <= LAYERS:
                    bias_h(0, k - 1)
                    gelus(0, k - 1)
                if 1 <= k <= CHUNKS:
                    copy_score_w(k - 1)
                if k == LN_ATTN:
                    qk_exps(0)
                    copy_num(0)
            copy_turned(0, 0)
            with act_e.Fori(0, BATCH - 1) as n:
                cycles(n, True)
            cycles(BATCH - 1, False)

        @block.vector
        def _(dve):
            v = nc.vector
            steps = [0]

            def step(ins):
                steps[0] += 1
                ins.then_inc(dve_done, 1)
                return steps[0]

            def after(n):
                dve.wait_ge(dve_done, n)

            def restart():
                dve.wait_ge(dve_done, steps[0])
                dve.sem_clear(dve_done)
                steps[0] = 0

            dve.sem_inc(applied, RING)
            dve.sem_inc(row_summed, RING)
            dve.sem_inc(scaled, 3)
            dve.sem_inc(sum_read, 1)
            dve.sem_inc(listed, 2)
            dve.sem_inc(tok_free, 2)
            dve.sem_inc(tok_ready, 1)
            dve.wait_ge(masks, 3)
            v.tensor_tensor(center[:, :], ident[:, :], mean_w[:, :], ALU.subtract).then_inc(consts, 1)
            dve.wait_ge(consts, 1)
            dve.wait_ge(first_loaded, 16 * len(FIRST_LOADS))

            def make_conv(layer):
                for i in range(layer * TAPS, (layer + 1) * TAPS):
                    last = v.tensor_scalar(dw[:, i, :], center[:, :], dw_s[:, i:i + 1], None, ALU.mult)
                last.then_inc(conv_ready, 1)

            def scale_w1(layer):
                v.tensor_scalar(w1[:, layer, :], w1[:, layer, :], lnw_s[:, layer:layer + 1], None, ALU.mult)\
                    .then_inc(w1_ready, 1)

            def add_ln_b(layer):
                dve.wait_ge(ln_b_made, layer + 1)
                cols = slice(layer * FBLK, (layer + 1) * FBLK)
                v.tensor_tensor(ln_b1[:, cols], bank_u[:, cols], b1_s[:, cols], ALU.add).then_inc(ln_b_read, 1)

            def split_bias(r):
                after(step(v.tensor_copy(part_s, bias_s)))
                step(v.tensor_tensor(bias_s, bias_s, part_s, ALU.subtract))
                mine = ident[0:3, r:r + 1]
                if r == 0:
                    s = step(v.tensor_scalar(score_b[:, :], part_s, mine, None, ALU.mult))
                else:
                    s = step(v.scalar_tensor_tensor(out=score_b[:, :], in0=part_s, scalar=mine, in1=score_b[:, :],
                                                    op0=ALU.mult, op1=ALU.add))
                after(s)

            def invert(m, k):
                dve.wait_ge(rooted, m * LNS + (k + 1))
                v.reciprocal(rstd[:, :], std[:, :]).then_inc(inverted, 1)

            def normalise(m, k):
                dst = qc if k == LN_PEER else xhat
                for i, p in enumerate(PARTS):
                    dve.wait_ge(shifted_in, m * 2 * LNS + (2 * k + i + 1))
                    dve.wait_ge(spread, m * 2 * LNS + (2 * k + i + 1))
                    v.tensor_tensor(dst[:, p], shift[:, p], spread_bank[i][:, 0:SEQ // 2], ALU.mult)\
                        .then_inc(normed, 1)

            def add_mlp(m, k):
                dve.wait_ge(biased, m * LAYERS + (k + 1))
                for i, w in enumerate(WIDE):
                    dve.wait_ge(projected, m * 2 * LAYERS + (2 * k + i + 1))
                    v.scalar_tensor_tensor(out=hin[:, w], in0=product_bank[i][:, 0:w.stop - w.start],
                                           scalar=gamma[:, k:k + 1], in1=hb[:, w],
                                           op0=ALU.mult, op1=ALU.add).then_inc(added, 1)

            def clamp_qk(m):
                dve.wait_ge(qkv_made, m + 1)
                q_in = bank_c[0][:, :]
                v.tensor_scalar(q_exp[:, :], q_in, vecs[:, 4:5], 0.0, ALU.add, ALU.min).then_inc(clamped, 1)
                for j in range(2):
                    last = step(v.tensor_tensor(
                        kvt[:, 2 * j:2 * j + 2, 0:2 * DIM],
                        bank_c[1 + j][:, :].rearrange("p (i d) -> p i d", i=2),
                        kv_b[:, :].unsqueeze(1).broadcast_to([P, 2, 2 * DIM]), ALU.add))
                after(last)
                v.tensor_scalar(k_exp[:, :, :], kvt[:, :, 0:DIM], 0.0, None, ALU.min).then_inc(clamped, 1)
                step(v.tensor_scalar(q_pos[:, :], q_in, vecs[:, 4:5], 0.0, ALU.add, ALU.max))
                step(v.tensor_scalar(k_pos[:, :, :], kvt[:, :, 0:DIM], 0.0, None, ALU.max))

            def elu_qk(m):
                dve.wait_ge(exped, m * 2 + 2)
                after(steps[0])
                v.tensor_tensor(q_elu[:, :], q_exp[:, :], q_pos[:, :], ALU.add)
                v.tensor_tensor(k_elu[:, :, :], k_exp[:, :, :], k_pos[:, :, :], ALU.add).then_inc(elued, 1)

            def mask_kv(m):
                dve.wait_ge(kv_summed, m + 1)
                s = step(v.tensor_copy(kv_sum[:, :], bank_b[:, DIM:DIM + 1]))
                v.tensor_tensor(kv_m[:, :], head_mask[:, :], bank_b[:, 0:DIM], ALU.mult)
                after(s)
                v.tensor_scalar(ks_m[:, :], head_mask[:, 0:P:HDIM], kv_sum[:, :], None, ALU.mult)\
                    .then_inc(kv_masked, 1)

            def invert_den(m):
                dve.wait_ge(mix_made, m * 2 + 2)
                s = step(v.tensor_scalar(den[:, :], bank_c[2][:, 0:TILES * HEADS], 1e-6, None, ALU.add))
                after(s)
                s = step(v.reciprocal(inv_den[:, :], den[:, :]))
                after(s)
                v.tensor_copy(inv_wide[:, :].rearrange("p (i d) -> p i d", d=HDIM),
                              inv_den[:, :].unsqueeze(2).broadcast_to([P, TILES * HEADS, HDIM]))\
                    .then_inc(den_inverted, 1)

            def divide(m):
                dve.wait_ge(num_copied, m + 1)
                dve.wait_ge(den_spread, m + 1)
                v.tensor_tensor(mixed[:, :], q_pos[:, :], bank_c[2][:, :], ALU.mult).then_inc(mix_done, 1)

            def add_attn(m):
                dve.wait_ge(out_made, m + 1)
                v.scalar_tensor_tensor(out=h2[:, :], in0=bank_c[0][:, :], scalar=vecs[:, 5:6], in1=hf[:, :],
                                       op0=ALU.add, op1=ALU.add).then_inc(h2_done, 1)

            def lists(m, tile, c):
                dve.wait_ge(scored, m * (TILES * CHUNKS) + (tile * CHUNKS + c + 1))
                dve.sem_inc(passed, 1)
                after(steps[0])
                for hd in range(2):
                    for cc in range(2):
                        cols = bank_s[c % 2][:, (2 * hd + cc) * NKEY:(2 * hd + cc + 1) * NKEY]
                        s = step(v.max(half[:, cc, hd, 0, :], cols))
                for hd in range(2):
                    for cc in range(2):
                        cols = bank_s[c % 2][:, (2 * hd + cc) * NKEY:(2 * hd + cc + 1) * NKEY]
                        after(s - 3 + 2 * hd + cc)
                        last = v.max_index(half_u[:, hd, cc, :], half[:, cc, hd, 0, :], cols)
                        if hd == 1 and cc == 1:
                            last.then_inc(listed, 1)

            def pairs(m, tile, c):
                dve.wait_ge(listed, m * (TILES * CHUNKS) + (tile * CHUNKS + c + 3))
                step(v.tensor_scalar(half[:, 0, :, 1, :], half_u[:, :, 0, :], float(NKEY), None, ALU.mult))
                s = step(v.tensor_scalar(half[:, 1, :, 1, :], half_u[:, :, 1, :], 1.0, None, ALU.mult))
                after(s)
                a = half[:, 0, :, :, :].rearrange("p h w k -> p (h w) k")
                b = half[:, 1, :, :, :].rearrange("p h w k -> p (h w) k")
                cd = cand[:, :, :, :].rearrange("p h w k -> p (h w) k")
                step(v.tensor_tensor(cd[:, :, 0:8], a[:, :, 0:1].broadcast_to([P, 4, 8]), b[:, :, 0:8], ALU.add))
                step(v.tensor_tensor(cd[:, :, 8:12], a[:, :, 1:2].broadcast_to([P, 4, 4]), b[:, :, 0:4], ALU.add))
                step(v.tensor_tensor(cd[:, :, 12:16].rearrange("p w (a b) -> p w a b", a=2),
                                     a[:, :, 2:4].unsqueeze(3).broadcast_to([P, 4, 2, 2]),
                                     b[:, :, 0:2].unsqueeze(2).broadcast_to([P, 4, 2, 2]), ALU.add))
                s = step(v.tensor_tensor(cd[:, :, 16:20], a[:, :, 4:8], b[:, :, 0:1].broadcast_to([P, 4, 4]),
                                         ALU.add))
                after(s)
                for hd in range(2):
                    s = step(v.max(best[:, 2 * c + hd, :], cand[:, hd, 0, :]))
                for hd in range(2):
                    after(s - 1 + hd)
                    last = step(v.max_index(pos[:, hd, :], best[:, 2 * c + hd, :], cand[:, hd, 0, :]))
                after(last)
                s = step(v.tensor_tensor(
                    hit[:, :, :], pos[:, :, :].rearrange("p h k -> p (h k)").unsqueeze(2).broadcast_to([P, 16, CAND]),
                    cand_iota[:, :].unsqueeze(1).broadcast_to([P, 16, CAND]), ALU.is_equal))
                after(s)
                s = step(v.tensor_tensor(
                    picked[:, :, :].rearrange("p (h k) c -> p h k c", h=2),
                    hit[:, :, :].rearrange("p (h k) c -> p h k c", h=2),
                    cand[:, :, 1, :].unsqueeze(2).broadcast_to([P, 2, TOPK, CAND]), ALU.mult))
                after(s)
                with nc.allow_low_precision(reason="one whole number under 2^14 and zeros"):
                    v.tensor_reduce(expert[:, tile % 2, 16 * c:16 * c + 16], picked[:, :, :], AX.X, ALU.add)\
                        .then_inc(chosen, 1)

            def soften(m, tile):
                after(steps[0])
                v.tensor_tensor(shifted[:, :, :], best[:, :, :], best[:, :, 0:1].broadcast_to([P, PH, TOPK]),
                                ALU.subtract).then_inc(shift_done, 1)
                dve.wait_ge(exp_done, m * TILES + (tile + 1))
                s = step(v.tensor_reduce(total[:, :], expd[:, :, :], AX.X, ALU.add))
                after(s)
                s = step(v.reciprocal(inv_total[:, :], total[:, :]))
                after(s)
                w = weight[:, tile % 2, :].rearrange("p (h k) -> p h k", h=PH)
                s = step(v.tensor_tensor(w, expd[:, :, :], inv_total[:, :].unsqueeze(2).broadcast_to([P, PH, TOPK]),
                                         ALU.mult))
                after(s)
                step(v.tensor_scalar(weight[:, tile % 2, :], weight[:, tile % 2, :], 0.5, None, ALU.mult))

            def dots(n, slot):
                tile, r = slot // PH, slot % RING
                dve.wait_ge(landed[r], n * (SLOTS // RING * 16 * TOPK) + (slot // RING + 1) * 16 * TOPK)
                if slot % PH == 0:
                    dve.wait_ge(tok_ready, n * TILES + (tile + 2))
                pair = slot // 2
                d = dot[:, pair % 2, :]
                for k in range(TOPK):
                    col = slot % 2 * TOPK + k
                    s = step(v.tensor_tensor_reduce(ring[:, r, k, 0:DIM], ring[:, r, k, 0:DIM], tok[:, tile % 2, 0:DIM],
                                                    1.0, 0.0, ALU.mult, ALU.add, d[:, col:col + 1]))
                if slot % 2:
                    after(s)
                    s = step(v.tensor_tensor(dot2[:, :], d, d, ALU.mult))
                    after(s)
                    s = step(v.tensor_scalar(cubic[:, :], dot2[:, :], 0.044715, 1.0, ALU.mult, ALU.add))
                    after(s)
                    v.tensor_tensor(tanh_in[:, pair % 2, :], cubic[:, :], d, ALU.mult).then_inc(tanh_ready, 1)

            def apply(n, slot):
                tile, head, r, pair = slot // PH, slot % PH, slot % RING, slot // 2
                if slot % 2 == 0:
                    dve.wait_ge(tanh_done, n * (SLOTS // 2) + (pair + 1))
                    s = step(v.scalar_tensor_tensor(out=gated[:, :], in0=tanh[:, pair % 2, :], scalar=1.0,
                                                    in1=dot[:, pair % 2, :], op0=ALU.add, op1=ALU.mult))
                    dve.wait_ge(scaled, n * SLOTS + (slot + 1))
                    after(s)
                    v.tensor_tensor(val[:, pair % 2, :], gated[:, :],
                                    weight[:, tile % 2, head * TOPK:(head + 2) * TOPK], ALU.mult).then_inc(val_ready, 1)
                dve.wait_ge(val_ready, n * (SLOTS // 2) + (pair + 1))
                after(steps[0])
                for k in range(ON_DVE):
                    up, a = ring[:, r, k, DIM:2 * DIM], val[:, pair % 2, slot % 2 * TOPK + k:slot % 2 * TOPK + k + 1]
                    if head == 0:
                        last = v.tensor_scalar(acc[:, k, :], up, a, None, ALU.mult)
                    else:
                        last = v.scalar_tensor_tensor(out=acc[:, k, :], in0=up, scalar=a, in1=acc[:, k, :],
                                                      op0=ALU.mult, op1=ALU.add)
                    if k < ON_DVE - 1:
                        step(last)
                last.then_inc(applied, 1)
                dve.wait_ge(applied, n * SLOTS + (slot + 1 + RING))
                if head == PH - 1:
                    step(v.tensor_reduce(summed_d[:, :], acc[:, :, :].rearrange("p k d -> p d k"), AX.X, ALU.add))

            def finish(n, tile):
                s = steps[0]
                dve.wait_ge(row_summed, n * SLOTS + ((tile + 1) * PH + RING))
                v.tensor_reduce(summed_t[:, :], bank_u[:, :].rearrange("p (k d) -> p d k", d=DIM), AX.X, ALU.add)\
                    .then_inc(sum_read, 1)
                after(s)
                dve.wait_ge(sum_read, n * TILES + (tile + 2))
                s = step(v.tensor_tensor(summed[:, :], summed_d[:, :], summed_t[:, :], ALU.add))
                if tile >= 2:
                    dve.wait_ge(out_free[tile % 2], n * 32 + 16)
                else:
                    dve.wait_ge(out_free[tile % 2], n * 32)
                after(s)
                v.tensor_tensor(outt[:, tile % 2, :], summed[:, :], tok[:, tile % 2, DIM:2 * DIM], ALU.add)\
                    .then_inc(out_ready, 1)
                dve.wait_ge(out_ready, n * TILES + (tile + 1))
                dve.sem_inc(tok_free, 1)

            def cycle(n, c, more):
                m = n + 1
                k = LN_AT.get(c) if more else None
                attn = more and c == ATTN_AT
                dots(n, 2 * c)
                if attn:
                    clamp_qk(m)
                dots(n, 2 * c + 1)
                if attn:
                    elu_qk(m)
                if paired_in(c, more):
                    ahead, tile, chunk = paired_in(c, more)
                    pairs(n + ahead, tile, chunk)
                if c % CHUNKS == 0:
                    soften(n, c // CHUNKS)
                if k is not None:
                    invert(m, k)
                if attn:
                    mask_kv(m)
                apply(n, 2 * c)
                if k is not None:
                    normalise(m, k)
                if attn:
                    invert_den(m)
                if listed_in(c, more):
                    ahead, tile, chunk = listed_in(c, more)
                    lists(n + ahead, tile, chunk)
                if more and c == LN_ATTN_AT:
                    invert(m, LN_ATTN)
                if attn:
                    divide(m)
                apply(n, 2 * c + 1)
                if c % CHUNKS == 0 and c:
                    finish(n, c // CHUNKS - 1)
                if more and c in MLP_AT:
                    add_mlp(m, MLP_AT[c])
                if more and c == LN_ATTN_AT:
                    normalise(m, LN_ATTN)
                if attn:
                    add_attn(m)

            def cycles(n, more):
                for c in range(CYCLES):
                    cycle(n, c, more)
                finish(n, TILES - 1)

            step(v.memset(ones_b[:, :], 1.0))
            make_conv(0)
            for k in range(LNS):
                invert(0, k)
                normalise(0, k)
                if k == 0:
                    v.tensor_tensor(gamma_b2[:, :], gamma[:, :], b2_s, ALU.mult)
                elif k < LAYERS:
                    make_conv(k)
                if k < LAYERS:
                    add_ln_b(k)
                    scale_w1(k)
                if 1 <= k <= LAYERS:
                    add_mlp(0, k - 1)
                if k == CHUNKS:
                    dve.wait_ge(score_w_copied, CHUNKS)
                if CHUNKS <= k < CHUNKS + 3:
                    split_bias(k - CHUNKS)
                if k == CHUNKS + 3:
                    dve.sem_inc(score_b_ready, 1)
                if k == LN_ATTN:
                    clamp_qk(0)
                    elu_qk(0)
                    mask_kv(0)
                    invert_den(0)
                    divide(0)
                    add_attn(0)
            for c in range(CHUNKS):
                lists(0, 0, c)
                if c < CHUNKS - 1:
                    pairs(0, 0, c)
            restart()
            with dve.Fori(0, BATCH - 1) as n:
                cycles(n, True)
                restart()
            cycles(BATCH - 1, False)


def kernel(x, L0_tok_embed_w, L0_tok_embed_b, L0_tok_norm_w, L0_tok_norm_b, L0_tok_dw_w, L0_tok_dw_b,
           L0_tok_ln_w, L0_tok_ln_b, L0_tok_w1, L0_tok_b1, L0_tok_w2, L0_tok_b2, L0_tok_gamma,
           L0_tok_final_ln_w, L0_tok_final_ln_b, L0_attn_Wq, L0_attn_bq, L0_attn_Wk, L0_attn_bk,
           L0_attn_Wv, L0_attn_bv, L0_attn_Wo, L0_attn_bo, L0_ffn_Wq, L0_ffn_bq, L0_ffn_keys,
           L0_ffn_w_down_embed, L0_ffn_w_up_embed):
    import numpy as np
    import concourse.bacc as bacc
    from concourse.bass_utils import run_bass_kernel_spmd

    f = np.asarray
    zeros = np.zeros((LNS - 1 - LAYERS, DIM), np.float32)
    layouts = {
        "x": f(x),
        "embed_w": f(L0_tok_embed_w),
        "conv_b": np.concatenate([f(L0_tok_embed_b)[None], f(L0_tok_dw_b), zeros]).T,
        "dw_w": f(L0_tok_dw_w)[:, :, 0, :].transpose(1, 0, 2).reshape(DIM, LAYERS * TAPS),
        "ln_w": f(L0_tok_ln_w).T,
        "ln_b": f(L0_tok_ln_b).T,
        "w1": f(L0_tok_w1).transpose(2, 0, 1),
        "b1": f(L0_tok_b1).reshape(LAYERS * FBLK, P).T,
        "w2": f(L0_tok_w2).transpose(2, 0, 1).reshape(FBLK, P, LAYERS, DIM).transpose(1, 2, 0, 3)
                          .reshape(P, LAYERS * FBLK, DIM),
        "b2": f(L0_tok_b2).T,
        "gamma": f(L0_tok_gamma).T,
        "wq": f(L0_attn_Wq).T,
        "wkv": np.concatenate([f(L0_attn_Wk), f(L0_attn_Wv)]).T,
        "bkv": np.concatenate([f(L0_attn_bk), f(L0_attn_bv)])[None],
        "wo": f(L0_attn_Wo).T,
        "vecs": np.stack([f(L0_tok_norm_w), f(L0_tok_norm_b), f(L0_tok_final_ln_w), f(L0_tok_final_ln_b),
                          f(L0_attn_bq), f(L0_attn_bo)], axis=1),
        "ffn_wq": f(L0_ffn_Wq).reshape(2 * PH, HALF, DIM).transpose(1, 0, 2),
        "ffn_bq": f(L0_ffn_bq).reshape(2 * PH, HALF).T,
        "keys": f(L0_ffn_keys).reshape(2 * PH, NKEY, HALF).transpose(2, 0, 1),
        "experts": np.concatenate([f(L0_ffn_w_down_embed), f(L0_ffn_w_up_embed)], axis=1),
    }
    arrays = {"in_" + name: np.ascontiguousarray(a) for name, a in layouts.items()}
    nc = bacc.Bacc("TRN2", target_bir_lowering=False, num_devices=1)
    t = {name: nc.dram_tensor("in_" + name, a.shape, mybir.dt.from_np(a.dtype), kind="ExternalInput").ap()
         for name, a in layouts.items()}
    out = nc.dram_tensor("out", (BATCH, SEQ, DIM), F32, kind="ExternalOutput").ap()
    build(nc, t, out)
    r = run_bass_kernel_spmd(nc, [arrays], core_ids=[0])
    return r.results[0]["out"]
```
